# Optimizing a Trainium2 kernel written in Bass

```python
import numpy as np
import jax
import jax.numpy as jnp

def _softmax(x, axis=-1):
    return jax.nn.softmax(x, axis=axis)

def _gelu(x):
    return jax.nn.gelu(x, approximate=True)

def _silu(x):
    return jax.nn.silu(x)

def _sigmoid(x):
    return jax.nn.sigmoid(x)

def _layernorm(x, axis=-1, eps=1e-05):
    m = jnp.mean(x, axis=axis, keepdims=True)
    v = jnp.var(x, axis=axis, keepdims=True)
    return (x - m) / jnp.sqrt(v + eps)

def _scatter_add(tgt, idx, src, axis=0):
    return tgt.at[idx].add(src)

def _segment_sum(src, seg, n):
    return jax.ops.segment_sum(src, seg, n)
kernel_name = 'mk_adj_resnorm_d1_adj_r2_ec7791'

def setup_inputs(seed: int=0):
    np.random.seed(seed)
    _w = jnp.asarray

    def _rec_inputs():
        import jax
        import jax.numpy as jnp
        _gk = jax.random.key(seed)
        x = -9.806e-05 + 1 * jax.random.normal(jax.random.fold_in(_gk, 1), (4096, 64), jnp.float32)
        _a = jax.random.bernoulli(jax.random.fold_in(_gk, 2), 0.000488281, (4096, 4096))
        adj = _a.astype(jnp.int32)
        return (x, adj)
    x, adj = _rec_inputs()

    def _L0_gnn_setup():
        import jax, jax.numpy as jnp
        import numpy as np
        ALPHA = 0.2
        NEG_BIG = -9000000000000000.0
        key = jax.random.key(seed)
        k1, k2, k3, k4, k5 = jax.random.split(key, 5)
        N, M, F_in, F_out = (4096, 4096, 64, 64)
        item_embs = jax.random.normal(k1, (N, F_in), dtype=jnp.float32)
        entity_embs = jax.random.normal(k2, (M, F_in), dtype=jnp.float32)
        adj = jax.random.randint(k3, (N, M), 0, 2, dtype=jnp.int32)
        W = jax.random.normal(k4, (F_in, F_out), dtype=jnp.float32)
        a = jax.random.normal(k5, (2 * F_out, 1), dtype=jnp.float32)
        return {'item_embs': item_embs, 'entity_embs': entity_embs, 'adj': adj, 'W': W, 'a': a}
    _L0_gnn_all = _L0_gnn_setup()
    _L0_gnn_in = {k: v for k, v in _L0_gnn_all.items() if k in ('entity_embs', 'W', 'a')}
    del _L0_gnn_all
    return {'x': x, 'adj': adj, 'L0_gnn_entity_embs': _L0_gnn_in['entity_embs'], 'L0_gnn_W': _L0_gnn_in['W'], 'L0_gnn_a': _L0_gnn_in['a']}

def reference(x, adj, L0_gnn_entity_embs, L0_gnn_W, L0_gnn_a):
    import jax
    import jax.numpy as jnp

    def _L0_gnn_ref(item_embs, entity_embs, adj, W, a):
        import jax, jax.numpy as jnp
        import numpy as np
        ALPHA = 0.2
        NEG_BIG = -9000000000000000.0
        F_out = W.shape[1]
        Wh = item_embs @ W
        We = entity_embs @ W
        a1 = a[:F_out, 0]
        a2 = a[F_out:, 0]
        scores = (Wh @ a1)[:, None] + (We @ a2)[None, :]
        e = jnp.where(scores > 0, scores, ALPHA * scores)
        e = jnp.where(adj > 0, e, NEG_BIG)
        attention = jax.nn.softmax(e, axis=1)
        entity_emb_weighted = attention @ entity_embs
        h_prime = entity_emb_weighted + item_embs
        return jax.nn.elu(h_prime)
    x = _layernorm(x + _L0_gnn_ref(x, L0_gnn_entity_embs, adj, L0_gnn_W, L0_gnn_a), axis=-1)
    return x

_drawn_inputs = setup_inputs


def setup_inputs(seed=0):
    import zlib

    import numpy as np

    out = dict(_drawn_inputs(seed))
    spreads = {}
    factors = {}
    for name, (base, spread) in spreads.items():
        noise = np.random.default_rng([zlib.crc32(name.encode()), seed]).standard_normal(out[name].shape)
        drawn = base * np.exp(spread * noise) if base else spread * noise
        out[name] = jnp.asarray(drawn.astype(out[name].dtype))
    for name, factor in factors.items():
        out[name] = (out[name] * factor).astype(out[name].dtype)
    return out
```

```python
from contextlib import ExitStack

import concourse.bass as bass
from concourse import mybir

ALU = mybir.AluOpType
ACT = mybir.ActivationFunctionType
BF16 = mybir.dt.bfloat16
F32 = mybir.dt.float32
I32 = mybir.dt.int32
U16 = mybir.dt.uint16
AX_X = mybir.AxisListType.X
RMAX = bass.bass_isa.ReduceOp.max

P = 128
ALPHA = 0.2
EPS = 1e-5
WALL = 2.0 ** 90
LEVELS = 65000.0


def gat_layernorm(nc: bass.Bass, adj_t, x_t, x_rows, ent_t, ent_rows, w_t, a_cols, out):
    BLOCKS, PAIRS, _, _, IB = adj_t.shape
    F = ent_t.shape[0]
    TILES = 2 * PAIRS
    CH = IB // P
    NI, NJ = BLOCKS * IB, TILES * P
    C_ALL = NI // P
    FE = F + 2
    BANK = 512
    HALVES = IB // BANK
    LAG = 2
    RING = PAIRS + LAG + 2
    PEEL = 6
    PR = 4

    with ExitStack() as ctx:
        def sb(name, shape, dt):
            return ctx.enter_context(nc.sbuf_tensor(name, shape, dt))

        def sem(name):
            return ctx.enter_context(nc.semaphore(name))

        aux = ctx.enter_context(nc.psum_tensor("aux", [P, 4 * BANK], F32))
        numer = [ctx.enter_context(nc.psum_tensor(f"numer{i}", [P, IB], F32)) for i in range(2)]

        adj_in = sb("adj_in", [P, 2, 2, IB], I32)
        walls = sb("walls", [P, RING * 2 * IB], BF16)
        level = sb("level", [P, 2, IB], U16)
        top = sb("top", [P, 2, IB], U16)
        topf = sb("topf", [P, IB], F32)
        diag_a = sb("diag_a", [P, CH, P], F32)
        diag_b = sb("diag_b", [P, CH, P], F32)
        row_a = sb("row_a", [P, IB], F32)
        row_b = sb("row_b", [P, IB], F32)
        z = sb("z", [P, 2, IB], F32)
        masked = sb("masked", [P, 2, IB], F32)
        prob = sb("prob", [P, PR, IB], F32)
        ent = sb("ent", [P, TILES * FE], F32)
        ent3 = ent[:, :].rearrange("p (t f) -> p t f", f=FE)
        xr = sb("xr", [P, C_ALL, F], F32)
        numer_sb = sb("numer_sb", [P, IB], F32)
        ident = sb("ident", [P, P], F32)
        ones = sb("ones", [P, P], F32)
        wt = sb("wt", [F, F], F32)
        ac = sb("ac", [F, 2], F32)
        wa = sb("wa", [F, 2], F32)
        s2 = sb("s2", [P, TILES], F32)
        s2_08 = sb("s2_08", [P, TILES], F32)
        s2_02 = sb("s2_02", [P, TILES], F32)
        s2_lev = sb("s2_lev", [P, TILES], F32)
        s1 = sb("s1", [P, C_ALL], F32)
        ext = sb("ext", [P, 2], F32)
        gext = sb("gext", [P, 2], F32)
        sc = sb("sc", [P, 4], F32)
        q = sb("q", [P, CH], F32)
        mu = sb("mu", [P, CH], F32)
        sm = sb("sm", [P, CH], F32)
        mx = sb("mx", [P, CH], F32)
        col_a = sb("col_a", [P, CH], F32)
        col_b = sb("col_b", [P, CH], F32)
        bare = sb("bare", [P, C_ALL], F32)
        ent_sum = sb("ent_sum", [P, FE], F32)
        uniform = sb("uniform", [P, CH, FE], F32)
        fs = sb("fs", [P, CH, FE], F32)
        rden = sb("rden", [P, CH], F32)
        h = sb("h", [P, CH, F], F32)
        neg = sb("neg", [P, CH, F], F32)
        eneg = sb("eneg", [P, CH, F], F32)
        y = sb("y", [P, CH, F], F32)
        sq = sb("sq", [P, CH, F], F32)
        mean = sb("mean", [P, CH], F32)
        var = sb("var", [P, CH], F32)
        rstd = sb("rstd", [P, CH], F32)
        wall_col = sb("wall_col", [P, 1], F32)
        half = sb("half", [P, CH], F32)
        yout = sb("yout", [P, CH, F], F32)

        tview = walls[:, (RING - 8) * 2 * IB:RING * 2 * IB].bitcast(F32)
        entT = tview[0:F, 0:NJ]
        xT = tview[0:F, NJ:NJ + NI]

        adj_loaded = [sem(f"adj_loaded{i}") for i in range(2)]
        w_loaded = sem("w_loaded")
        entT_loaded = sem("entT_loaded")
        xT_loaded = sem("xT_loaded")
        ent_loaded = sem("ent_loaded")
        x_loaded = sem("x_loaded")
        out_stored = sem("out_stored")
        ones_made = sem("ones_made")
        ident_zero = sem("ident_zero")
        ident_made = sem("ident_made")
        pad_made = sem("pad_made")
        wall_made = sem("wall_made")
        half_made = sem("half_made")
        wa_mm = sem("wa_mm")
        wa_made = sem("wa_made")
        s2_mm = sem("s2_mm")
        s1_mm = sem("s1_mm")
        sum_mm = sem("sum_mm")
        setup = sem("setup")
        ext_made = sem("ext_made")
        gext_made = sem("gext_made")
        sum_made = sem("sum_made")
        walls_made = sem("walls_made")
        level_made = sem("level_made")
        top_made = sem("top_made")
        z_made = sem("z_made")
        masked_made = sem("masked_made")
        prob_made = sem("prob_made")
        prob_used = sem("prob_used")
        topf_made = sem("topf_made")
        topT_made = sem("topT_made")
        col = sem("col")
        diag_made = sem("diag_made")
        rows_mm = sem("rows_mm")
        rows_made = sem("rows_made")
        numer_copied = sem("numer_copied")
        numerT_made = sem("numerT_made")
        uniform_made = sem("uniform_made")
        fin = sem("fin")
        eneg_made = sem("eneg_made")
        sq_made = sem("sq_made")
        rstd_made = sem("rstd_made")

        COLS = 7
        FINS = 13
        NEG_AT, Y_AT, VAR_AT = 5, 10, 12

        def slot(g, hh=0, n=2):
            s = (g % RING) * (2 * IB)
            return walls[:, bass.ds(s + hh * IB, n * IB)]

        def steps(eng, do):
            for k in range(BLOCKS + 2):
                for u in range(PEEL):
                    do(k, u)
                if k <= BLOCKS:
                    with eng.Fori(PEEL // 2, PAIRS // 2) as w:
                        do(k, w * 2)
                        do(k, w * 2 + 1, 1)

        def second(k, u):
            early = isinstance(u, int) and u < LAG
            b, v = (k - 2, u + PAIRS - LAG) if early else (k - 1, u - LAG)
            return (b, v) if 0 <= b < BLOCKS else None

        block = ctx.enter_context(nc.Block())

        @block.sync
        def _(sp):
            sp.dma_start(wt[:, :], w_t).then_inc(w_loaded, 16)
            sp.dma_start(ac[:, :], a_cols).then_inc(w_loaded, 16)
            sp.dma_start(entT, ent_t).then_inc(entT_loaded, 16)

            def load(k, u, odd):
                if not (k == 0 and isinstance(u, int) and u < 2):
                    sp.wait_ge(walls_made, PAIRS * k + u - 1)
                src = adj_t[k, bass.ds(u, 1)].rearrange("a p t i -> (a p) t i")
                sp.dma_start(adj_in[:, odd], src).then_inc(adj_loaded[odd], 16)

            load(0, 0, 0)
            sp.dma_start(xT, x_t).then_inc(xT_loaded, 16)
            load(0, 1, 1)
            sp.dma_start(ent3[:, :, 0:F], ent_rows).then_inc(ent_loaded, 16)
            sp.dma_start(xr[:, :, :], x_rows).then_inc(x_loaded, 16)
            for k in range(BLOCKS + 2):
                if k < BLOCKS:
                    with sp.Fori(1 if k == 0 else 0, PAIRS // 4) as w:
                        load(k, w * 2, 0)
                        load(k, w * 2 + 1, 1)
                if k >= 2:
                    b = k - 2
                    sp.wait_ge(fin, FINS * (b + 1))
                    sp.dma_start(out[:, b * CH:(b + 1) * CH, :], yout[:, :, :]).then_inc(out_stored, 16)
                if k < BLOCKS:
                    with sp.Fori(PAIRS // 4, PAIRS // 2) as w:
                        load(k, w * 2, 0)
                        load(k, w * 2 + 1, 1)
            sp.wait_ge(out_stored, 16 * BLOCKS)

        @block.scalar
        def _(act):
            def step(k, u, odd=None):
                odd = u % 2 if odd is None and isinstance(u, int) else (odd or 0)
                g = PAIRS * k + u
                if k < BLOCKS:
                    act.wait_ge(adj_loaded[odd], 16 * (PAIRS // 2 * k + 1) + 8 * (u - odd))
                    if k >= 2 or (k == 1 and not (isinstance(u, int) and u < RING - PAIRS)):
                        act.wait_ge(masked_made, 2 * (g - RING + 1))
                    nc.scalar.activation(slot(g), adj_in[:, odd].rearrange("p t i -> p (t i)"), ACT.Relu,
                                         bias=wall_col[:, :], scale=-WALL).then_inc(walls_made, 1)
                if second(k, u):
                    b, v = second(k, u)
                    for t in range(2):
                        n = TILES * b + 2 * v + t
                        act.wait_ge(masked_made, n + 1)
                        if not (b == 0 and isinstance(v, int) and v < PR // 2):
                            act.wait_ge(prob_used, n + 1 - PR)
                        nc.scalar.activation(prob[:, 2 * odd + t], masked[:, t], ACT.Exp,
                                             bias=s2_02[:, bass.ds(2 * v + t, 1)]).then_inc(prob_made, 1)
                if 1 <= k <= BLOCKS and isinstance(u, int) and u == 1:
                    act.wait_ge(rows_mm, k)
                    nc.scalar.copy(row_a[:, :], aux[:, 0:IB]).then_inc(rows_made, 1)
                    nc.scalar.copy(row_b[:, :], aux[:, IB:2 * IB]).then_inc(rows_made, 1)
                if k >= 2 and isinstance(u, int):
                    b = k - 2
                    if u == 2:
                        act.wait_ge(prob_used, TILES * (b + 1))
                        if b >= 1:
                            act.wait_ge(numerT_made, b)
                        nc.scalar.copy(numer_sb[0:FE, :], numer[b % 2][0:FE, :]).then_inc(numer_copied, 1)
                    if u == 3:
                        act.wait_ge(fin, FINS * b + NEG_AT)
                        nc.scalar.activation(eneg[:, :, :], neg[:, :, :], ACT.Exp).then_inc(eneg_made, 1)
                    if u == 4:
                        act.wait_ge(fin, FINS * b + Y_AT)
                        nc.scalar.activation(sq[:, :, :], y[:, :, :], ACT.Square).then_inc(sq_made, 1)
                if k == 0 and isinstance(u, int) and u == PEEL - 1:
                    act.wait_ge(s1_mm, 1)

            act.wait_ge(wall_made, 1)
            steps(act, step)

        @block.gpsimd
        def _(pool):
            nc.gpsimd.memset(ident[:, :], 0.0).then_inc(ident_zero, 1)
            pool.wait_ge(ident_zero, 1)
            nc.gpsimd.affine_select(out=ident[:, :], in_=ident[:, :], compare_op=ALU.not_equal, fill=1.0, base=0,
                                    pattern=[[-1, P]], channel_multiplier=1).then_inc(ident_made, 1)
            nc.gpsimd.memset(ent3[:, :, F:FE], 1.0).then_inc(pad_made, 1)
            nc.gpsimd.memset(half[:, :], -0.5).then_inc(half_made, 1)
            pool.wait_ge(ext_made, 2)
            nc.gpsimd.partition_all_reduce(gext[:, :], ext[:, :], P, RMAX).then_inc(gext_made, 1)

            def step(k, u, odd=None):
                odd = u % 2 if odd is None and isinstance(u, int) else (odd or 0)
                if k >= 2 and isinstance(u, int) and u == 3:
                    b = k - 2
                    pool.wait_ge(sum_made, 1)
                    pool.wait_ge(col, COLS * (b + 1))
                    nc.gpsimd.tensor_tensor(uniform[:, :, :],
                                            bare[:, b * CH:(b + 1) * CH].unsqueeze(2).to_broadcast([P, CH, FE]),
                                            ent_sum[:, :].unsqueeze(1).to_broadcast([P, CH, FE]),
                                            ALU.mult).then_inc(uniform_made, 1)
                if second(k, u):
                    b, v = second(k, u)
                    for t in range(2):
                        n = TILES * b + 2 * v + t
                        pool.wait_ge(z_made, n + 1)
                        if not (b == 0 and isinstance(v, int) and v == 0):
                            pool.wait_ge(prob_made, n - 1)
                        nc.gpsimd.tensor_tensor(masked[:, t], z[:, t], slot(PAIRS * b + v, t, 1),
                                                ALU.subtract).then_inc(masked_made, 1)
                if k >= 2 and isinstance(u, int) and u == 5:
                    b = k - 2
                    pool.wait_ge(fin, FINS * b + VAR_AT)
                    nc.gpsimd.tensor_tensor(rstd[:, :], var[:, :], half[:, :], ALU.pow).then_inc(rstd_made, 1)

            steps(pool, step)

        @block.vector
        def _(dve):
            n_setup = [0]

            def link(ins):
                n_setup[0] += 1
                ins.then_inc(setup, 1)
                dve.wait_ge(setup, n_setup[0])

            nc.vector.memset(wall_col[:, :], WALL).then_inc(wall_made, 1)
            nc.vector.memset(ones[:, :], 1.0).then_inc(ones_made, 1)
            dve.wait_ge(wa_mm, 1)
            nc.vector.tensor_copy(wa[:, :], aux[0:F, BANK:BANK + 2]).then_inc(wa_made, 1)
            dve.wait_ge(s2_mm, 1)
            link(nc.vector.tensor_copy(s2[:, :], aux[:, 0:TILES]))
            nc.vector.tensor_reduce(ext[:, 0:1], s2[:, :], AX_X, ALU.max).then_inc(ext_made, 1)
            link(nc.vector.tensor_scalar(s2_lev[:, :], s2[:, :], -1.0, None, ALU.mult))
            nc.vector.tensor_reduce(ext[:, 1:2], s2_lev[:, :], AX_X, ALU.max).then_inc(ext_made, 1)
            nc.vector.tensor_scalar(s2_08[:, :], s2[:, :], 1.0 - ALPHA, None, ALU.mult)
            link(nc.vector.tensor_scalar(s2_02[:, :], s2[:, :], ALPHA, None, ALU.mult))
            dve.wait_ge(gext_made, 1)
            link(nc.vector.tensor_tensor(sc[:, 0:1], gext[:, 0:1], gext[:, 1:2], ALU.add))
            link(nc.vector.tensor_scalar(sc[:, 1:2], sc[:, 0:1], 1e-6, 1.0 / LEVELS, ALU.max, ALU.mult))
            link(nc.vector.reciprocal(sc[:, 2:3], sc[:, 1:2]))
            link(nc.vector.tensor_scalar(s2_lev[:, :], s2[:, :], gext[:, 1:2], sc[:, 2:3], ALU.add, ALU.mult))
            link(nc.vector.tensor_scalar(s2_lev[:, :], s2_lev[:, :], 1.0, None, ALU.add))
            dve.wait_ge(s1_mm, 1)
            link(nc.vector.tensor_copy(s1[:, :], aux[:, 3 * BANK:3 * BANK + C_ALL]))

            def top_ends(b):
                dve.wait_ge(top_made, (PAIRS - 1) * (b + 1))
                if b >= 1:
                    dve.wait_ge(topT_made, b)
                nc.vector.tensor_tensor(topf[:, :], top[:, 0], top[:, 1], ALU.max).then_inc(topf_made, 1)

            def columns(b):
                n = [COLS * b]

                def chain(ins):
                    n[0] += 1
                    ins.then_inc(col, 1)
                    dve.wait_ge(col, n[0])

                here = slice(b * CH, (b + 1) * CH)
                dve.wait_ge(topT_made, b + 1)
                chain(nc.vector.tensor_reduce(q[:, :], aux[:, 0:IB].rearrange("p (c j) -> p c j", j=P), AX_X, ALU.max))
                chain(nc.vector.tensor_scalar(bare[:, here], q[:, :], 0.0, None, ALU.is_equal))
                chain(nc.vector.tensor_scalar(mu[:, :], q[:, :], sc[:, 1:2], gext[:, 1:2], ALU.mult, ALU.subtract))
                chain(nc.vector.tensor_tensor(sm[:, :], mu[:, :], s1[:, here], ALU.add))
                chain(nc.vector.scalar_tensor_tensor(out=mx[:, :], in0=sm[:, :], scalar=ALPHA, in1=sm[:, :],
                                                     op0=ALU.mult, op1=ALU.max))
                chain(nc.vector.tensor_tensor(col_a[:, :], s1[:, here], mx[:, :], ALU.subtract))
                chain(nc.vector.scalar_tensor_tensor(out=col_b[:, :], in0=s1[:, here], scalar=ALPHA, in1=mx[:, :],
                                                     op0=ALU.mult, op1=ALU.subtract))
                if b == 0:
                    dve.wait_ge(ident_made, 1)
                else:
                    dve.wait_ge(rows_mm, b)
                for d, c in ((diag_a, col_a), (diag_b, col_b)):
                    nc.vector.tensor_tensor(d[:, :, :], ident[:, :].unsqueeze(1).to_broadcast([P, CH, P]),
                                            c[:, :].unsqueeze(2).to_broadcast([P, CH, P]),
                                            ALU.mult).then_inc(diag_made, 1)

            def finish(b, part):
                n = [FINS * b + {0: 0, 1: NEG_AT, 2: Y_AT}[part]]

                def chain(ins, hold=True):
                    n[0] += 1
                    ins.then_inc(fin, 1)
                    if hold:
                        dve.wait_ge(fin, n[0])

                wide = [P, CH, F]
                xs = xr[:, b * CH:(b + 1) * CH, :]
                if part == 0:
                    dve.wait_ge(numerT_made, b + 1)
                    dve.wait_ge(uniform_made, b + 1)
                    c2 = CH // 2
                    for a in range(1):
                        tr = aux[:, 0:2 * BANK].rearrange("p (a r) -> p a r", a=2)[:, :, 0:c2 * FE].rearrange(
                            "p a (c f) -> p a c f", f=FE)
                        chain(nc.vector.tensor_tensor(fs[:, :, :].rearrange("p (a c) f -> p a c f", a=2), tr,
                                                      uniform[:, :, :].rearrange("p (a c) f -> p a c f", a=2), ALU.add))
                    chain(nc.vector.reciprocal(rden[:, :].unsqueeze(2), fs[:, :, F:F + 1]))
                    chain(nc.vector.tensor_tensor(h[:, :, :], fs[:, :, 0:F], rden[:, :].unsqueeze(2).to_broadcast(wide),
                                                  ALU.mult))
                    if b == 0:
                        dve.wait_ge(x_loaded, 16)
                    chain(nc.vector.tensor_tensor(h[:, :, :], h[:, :, :], xs, ALU.add))
                    chain(nc.vector.tensor_scalar(neg[:, :, :], h[:, :, :], 0.0, None, ALU.min), hold=False)
                if part == 1:
                    dve.wait_ge(eneg_made, b + 1)
                    chain(nc.vector.scalar_tensor_tensor(out=h[:, :, :], in0=h[:, :, :], scalar=0.0, in1=eneg[:, :, :],
                                                         op0=ALU.max, op1=ALU.add))
                    chain(nc.vector.scalar_tensor_tensor(out=h[:, :, :], in0=h[:, :, :], scalar=-1.0, in1=xs,
                                                         op0=ALU.add, op1=ALU.add))
                    chain(nc.vector.tensor_reduce(mean[:, :], h[:, :, :], AX_X, ALU.add))
                    chain(nc.vector.tensor_scalar(mean[:, :], mean[:, :], 1.0 / F, None, ALU.mult))
                    chain(nc.vector.tensor_tensor(y[:, :, :], h[:, :, :], mean[:, :].unsqueeze(2).to_broadcast(wide),
                                                  ALU.subtract), hold=False)
                if part == 2:
                    dve.wait_ge(sq_made, b + 1)
                    chain(nc.vector.tensor_reduce(var[:, :], sq[:, :, :], AX_X, ALU.add))
                    chain(nc.vector.tensor_scalar(var[:, :], var[:, :], 1.0 / F, EPS, ALU.mult, ALU.add), hold=False)
                    dve.wait_ge(rstd_made, b + 1)
                    if b >= 1:
                        dve.wait_ge(out_stored, 16 * b)
                    chain(nc.vector.tensor_tensor(yout[:, :, :], y[:, :, :],
                                                  rstd[:, :].unsqueeze(2).to_broadcast(wide), ALU.mult), hold=False)

            def step(k, u, odd=None):
                g = PAIRS * k + u
                fixed = isinstance(u, int)
                if 1 <= k <= BLOCKS and fixed and u == 0:
                    top_ends(k - 1)
                if k < BLOCKS:
                    dve.wait_ge(walls_made, g + 1)
                    first = fixed and u == 0
                    dst = top if first else level
                    if first and k >= 1:
                        dve.wait_ge(topf_made, k)
                    if not first and not (k == 0 and fixed and u == 1):
                        dve.wait_ge(top_made, (PAIRS - 1) * k + u - 1)
                    for t in range(2):
                        nc.vector.tensor_scalar(dst[:, t], slot(g, t, 1), 0.0, s2_lev[:, bass.ds(2 * u + t, 1)],
                                                ALU.is_equal, ALU.mult).then_inc(level_made, 1)
                sec = second(k, u)
                for t in range(2):
                    if sec:
                        b, v = sec
                        n = TILES * b + 2 * v + t
                        if fixed and v == 0 and t == 0:
                            dve.wait_ge(rows_made, 2 * (b + 1))
                        if not (b == 0 and fixed and v == 0):
                            dve.wait_ge(masked_made, n - 1)
                        nc.vector.scalar_tensor_tensor(out=z[:, t], in0=row_a[:, :],
                                                       scalar=s2_08[:, bass.ds(2 * v + t, 1)], in1=row_b[:, :],
                                                       op0=ALU.add, op1=ALU.max).then_inc(z_made, 1)
                    if t == 0 and k < BLOCKS and not first:
                        dve.wait_ge(level_made, 2 * (g + 1))
                        nc.vector.tensor_tensor(top[:, :, :], top[:, :, :], level[:, :, :],
                                                ALU.max).then_inc(top_made, 1)
                if 1 <= k <= BLOCKS and fixed and u == 0:
                    columns(k - 1)
                if k >= 2 and fixed and 3 <= u <= 5:
                    finish(k - 2, u - 3)
                if k == 0 and fixed and u == 1:
                    dve.wait_ge(sum_mm, 1)
                    nc.vector.tensor_copy(ent_sum[:, :], aux[:, 2 * BANK:2 * BANK + FE]).then_inc(sum_made, 1)

            steps(dve, step)

        @block.tensor
        def _(pe):
            pe.wait_ge(w_loaded, 32)
            nc.tensor.matmul(aux[0:F, BANK:BANK + 2], wt[:, :], ac[:, :], start=True, stop=True).then_inc(wa_mm, 1)
            pe.wait_ge(wa_made, 1)
            pe.wait_ge(entT_loaded, 16)
            for t in range(TILES):
                mm = nc.tensor.matmul(aux[:, t:t + 1], entT[:, t * P:(t + 1) * P], wa[:, 1:2], start=True, stop=True)
            mm.then_inc(s2_mm, 1)
            pe.wait_ge(xT_loaded, 16)
            for t in range(C_ALL):
                mm = nc.tensor.matmul(aux[:, 3 * BANK + t:3 * BANK + t + 1], xT[:, t * P:(t + 1) * P], wa[:, 0:1],
                                      start=True, stop=True)
            mm.then_inc(s1_mm, 1)
            pe.wait_ge(ent_loaded, 16)
            pe.wait_ge(pad_made, 1)
            pe.wait_ge(ones_made, 1)
            for t in range(TILES):
                mm = nc.tensor.matmul(aux[:, 2 * BANK:2 * BANK + FE], ones[:, :], ent3[:, t, :],
                                      start=(t == 0), stop=(t == TILES - 1))
            mm.then_inc(sum_mm, 1)
            pe.wait_ge(ident_made, 1)

            def step(k, u, odd=None):
                fixed = isinstance(u, int)
                odd = u % 2 if odd is None and fixed else (odd or 0)
                if 1 <= k <= BLOCKS and fixed and u == 0:
                    b = k - 1
                    pe.wait_ge(topf_made, b + 1)
                    if b == 0:
                        pe.wait_ge(sum_made, 1)
                    if b >= 2:
                        pe.wait_ge(fin, FINS * (b - 2) + 1)
                    for c in range(CH):
                        mm = nc.tensor.transpose(aux[:, c * P:(c + 1) * P], topf[:, c * P:(c + 1) * P], ident[:, :])
                    mm.then_inc(topT_made, 1)
                if k >= 2 and fixed and u == 3:
                    b = k - 2
                    pe.wait_ge(numer_copied, b + 1)
                    if k <= BLOCKS:
                        pe.wait_ge(rows_made, 2 * k)
                    if b >= 1:
                        pe.wait_ge(fin, FINS * (b - 1) + 1)
                    for c in range(CH):
                        at = c // (CH // 2) * BANK + c % (CH // 2) * FE
                        mm = nc.tensor.transpose(aux[:, at:at + FE], numer_sb[0:FE, c * P:(c + 1) * P],
                                                 ident[0:FE, 0:FE])
                    mm.then_inc(numerT_made, 1)
                if second(k, u):
                    b, v = second(k, u)
                    first = fixed and v == 0
                    last = fixed and v == PAIRS - 1
                    for t in range(2):
                        pe.wait_ge(prob_made, TILES * b + 2 * v + t + 1)
                        if first and t == 0 and b >= 2:
                            pe.wait_ge(numer_copied, b - 1)
                        for i in range(HALVES):
                            mm = nc.tensor.matmul(numer[b % 2][0:FE, i * BANK:(i + 1) * BANK],
                                                  ent[:, bass.ds((2 * v + t) * FE, FE)],
                                                  prob[:, 2 * odd + t, i * BANK:(i + 1) * BANK],
                                                  start=first and t == 0, stop=last and t == 1)
                        mm.then_inc(prob_used, 1)
                if 1 <= k <= BLOCKS and fixed and u == 0:
                    b = k - 1
                    pe.wait_ge(diag_made, 2 * (b + 1))
                    for r, d in enumerate((diag_a, diag_b)):
                        dflat = d[:, :, :].rearrange("p c j -> p (c j)")
                        for i in range(HALVES):
                            mm = nc.tensor.matmul(aux[:, r * IB + i * BANK:r * IB + (i + 1) * BANK], ones[:, :],
                                                  dflat[:, i * BANK:(i + 1) * BANK], start=True, stop=True)
                    mm.then_inc(rows_mm, 1)

            for k in range(BLOCKS + 2):
                for u in range(PAIRS if k <= BLOCKS else PEEL):
                    step(k, u)


def kernel(x, adj, L0_gnn_entity_embs, L0_gnn_W, L0_gnn_a):
    import numpy as np
    import concourse.bacc as bacc
    from concourse.bass_utils import run_bass_kernel_spmd

    x, adj, ent, w, a = (np.asarray(v) for v in (x, adj, L0_gnn_entity_embs, L0_gnn_W, L0_gnn_a))
    n_i, n_j = adj.shape
    f = w.shape[1]
    ib = 1024
    arrays = {
        "adj_t": adj.reshape(n_i // ib, ib, n_j // 256, 2, 128).transpose(0, 2, 4, 3, 1),
        "x_t": x.T,
        "x_rows": x.reshape(n_i // 128, 128, f).transpose(1, 0, 2),
        "ent_t": ent.T,
        "ent_rows": ent.reshape(n_j // 128, 128, f).transpose(1, 0, 2),
        "w_t": w.T,
        "a_cols": a.reshape(2, f).T,
    }
    arrays = {k: np.ascontiguousarray(v) for k, v in arrays.items()}
    nc = bacc.Bacc("TRN2", target_bir_lowering=False, num_devices=1)
    args = {k: nc.dram_tensor(k, v.shape, mybir.dt.from_np(v.dtype), kind="ExternalInput").ap()
            for k, v in arrays.items()}
    out = nc.dram_tensor("out", (128, n_i // 128, f), F32, kind="ExternalOutput").ap()
    gat_layernorm(nc, out=out, **args)
    r = run_bass_kernel_spmd(nc, [arrays], core_ids=[0])
    return r.results[0]["out"].transpose(1, 0, 2).reshape(n_i, f)
```

```python
from contextlib import ExitStack

import concourse.bass as bass
from concourse import mybir

ALU = mybir.AluOpType
ACT = mybir.ActivationFunctionType
BF16 = mybir.dt.bfloat16
F32 = mybir.dt.float32
I32 = mybir.dt.int32
U16 = mybir.dt.uint16
AX_X = mybir.AxisListType.X
RMAX = bass.bass_isa.ReduceOp.max

P = 128
ALPHA = 0.2
EPS = 1e-5
WALL = 2.0 ** 90
LEVELS = 65000.0
WIDTHS = (512, 1024, 1024, 1024, 512)


def gat_layernorm(nc: bass.Bass, adj_t, x_t, x_rows, ent_t, ent_rows, w_t, a_cols, out):
    NJ, NI, F = 2 * ent_t.shape[1], 2 * x_t.shape[1], w_t.shape[0]
    WIDTH = WIDTHS
    BLOCKS, IB = len(WIDTH), max(WIDTH)
    START = [sum(WIDTH[:b]) for b in range(BLOCKS)]
    TILES = NJ // P
    PAIRS = TILES // 2
    CH = IB // P
    C_ALL = NI // P
    FE = F + 2
    BANK = 512
    BC = 4
    LAG = 4
    RING = PAIRS + LAG + 3
    AHEAD = 2
    PEEL = LAG + 8
    PR = 4

    with ExitStack() as ctx:
        def sb(name, shape, dt):
            return ctx.enter_context(nc.sbuf_tensor(name, shape, dt))

        def sem(name):
            return ctx.enter_context(nc.semaphore(name))

        aux = ctx.enter_context(nc.psum_tensor("aux", [P, 4 * BANK], F32))
        numer = [ctx.enter_context(nc.psum_tensor(f"numer{i}", [P, IB], F32)) for i in range(2)]

        adj_in = sb("adj_in", [P, 2, 2 * IB], I32)
        walls = sb("walls", [P, RING * 2 * IB], BF16)
        level = sb("level", [P, 2, IB], U16)
        top = sb("top", [P, 2, IB], U16)
        topf = sb("topf", [P, IB], F32)
        diag_a = topf[:, :].rearrange("p (c j) -> p c j", j=P)
        diag_b = sb("diag_b", [P, CH, P], F32)
        row_a = sb("row_a", [P, 2, IB], F32)
        row_b = sb("row_b", [P, 2, IB], F32)
        z = sb("z", [P, 4, IB], F32)
        masked = sb("masked", [P, 2, IB], F32)
        prob = sb("prob", [P, PR, IB], F32)
        ZR = 4
        ent = sb("ent", [P, TILES * FE], F32)
        ent3 = ent[:, :].rearrange("p (t f) -> p t f", f=FE)
        xr = sb("xr", [P, C_ALL, F], F32)
        numer_sb = diag_b[:, :, :].rearrange("p c j -> p (c j)")
        ident = sb("ident", [P, P], F32)
        ones = sb("ones", [P, P], F32)
        wt = sb("wt", [F, F], F32)
        ac = sb("ac", [F, 2], F32)
        wa = sb("wa", [P, 2], F32)
        s2 = sb("s2", [P, TILES], F32)
        s2_08 = sb("s2_08", [P, TILES], F32)
        s2_02 = sb("s2_02", [P, TILES], F32)
        s2_lev = sb("s2_lev", [P, TILES], F32)
        s1 = sb("s1", [P, C_ALL], F32)
        ext = sb("ext", [P, 2], F32)
        gext = sb("gext", [P, 2], F32)
        sc = sb("sc", [P, 4], F32)
        q = sb("q", [P, CH], F32)
        mu = sb("mu", [P, CH], F32)
        sm = sb("sm", [P, CH], F32)
        mx = sb("mx", [P, CH], F32)
        col_a = sb("col_a", [P, CH], F32)
        col_b = sb("col_b", [P, CH], F32)
        bare = sb("bare", [P, C_ALL], F32)
        ent_sum = sb("ent_sum", [P, FE], F32)
        uniform = sb("uniform", [P, CH, FE], F32)
        rden = sb("rden", [P, CH], F32)
        h = sb("h", [P, CH, F], F32)
        neg = sb("neg", [P, CH, F], F32)
        eneg = neg
        y = sb("y", [P, CH, F], F32)
        sq = neg
        mean = sb("mean", [P, CH], F32)
        var = sb("var", [P, CH], F32)
        rstd = sb("rstd", [P, CH], F32)
        wall_col = sb("wall_col", [P, 1], F32)
        half = sb("half", [P, CH], F32)
        yout = neg

        tview = walls[:, (RING - 4) * 2 * IB:RING * 2 * IB].bitcast(F32)
        entT = tview[:, 0:NJ // 2]
        xT = tview[:, NJ // 2:(NJ + NI) // 2]

        adj_loaded = [sem(f"adj_loaded{i}") for i in range(2)]
        w_loaded = sem("w_loaded")
        entT_loaded = sem("entT_loaded")
        xT_loaded = sem("xT_loaded")
        ent_loaded = sem("ent_loaded")
        ent_made = sem("ent_made")
        x_loaded = sem("x_loaded")
        out_stored = sem("out_stored")
        ones_made = sem("ones_made")
        ident_zero = sem("ident_zero")
        ident_made = sem("ident_made")
        pad_made = sem("pad_made")
        wall_made = sem("wall_made")
        half_made = sem("half_made")
        wa_mm = sem("wa_mm")
        wa_made = sem("wa_made")
        s2_mm = sem("s2_mm")
        s1_mm = sem("s1_mm")
        sum_mm = sem("sum_mm")
        setup = sem("setup")
        ext_made = sem("ext_made")
        gext_made = sem("gext_made")
        sum_made = sem("sum_made")
        walls_made = sem("walls_made")
        level_made = sem("level_made")
        top_made = sem("top_made")
        z_made = sem("z_made")
        masked_made = sem("masked_made")
        prob_made = sem("prob_made")
        prob_used = sem("prob_used")
        topf_made = sem("topf_made")
        topT_made = sem("topT_made")
        col = sem("col")
        diag_made = sem("diag_made")
        rows_mm = sem("rows_mm")
        rows_made = sem("rows_made")
        numer_copied = sem("numer_copied")
        numerT_made = sem("numerT_made")
        uniform_made = sem("uniform_made")
        fin = sem("fin")
        eneg_made = sem("eneg_made")
        sq_made = sem("sq_made")
        rstd_made = sem("rstd_made")

        COLS = 7
        FINS = 13
        NEG_AT, Y_AT, VAR_AT = 5, 10, 12

        def slot(b, v, t=0, n=2):
            s = ((PAIRS * b + v) % RING) * (2 * IB)
            return walls[:, bass.ds(s + t * WIDTH[b], n * WIDTH[b])]

        def score_cols(bank):
            return aux[:, bank * BANK:(bank + 2) * BANK].rearrange("p (h t) -> p h t", h=2)[:, :, 0:TILES // 2]

        def score_col(bank, t):
            return score_cols(bank)[:, t // (TILES // 2), t % (TILES // 2):t % (TILES // 2) + 1]

        def steps(eng, do):
            for k in range(BLOCKS + 2):
                for u in range(PEEL):
                    do(k, u)
                if k <= BLOCKS:
                    with eng.Fori(PEEL // 2, PAIRS // 2) as w:
                        do(k, w * 2)
                        do(k, w * 2 + 1, 1)

        def second(k, u, lag=LAG):
            early = isinstance(u, int) and u < lag
            b, v = (k - 2, u + PAIRS - lag) if early else (k - 1, u - lag)
            return (b, v) if 0 <= b < BLOCKS else None

        block = ctx.enter_context(nc.Block())

        @block.sync
        def _(sp):
            sp.dma_start(wt[:, :], w_t).then_inc(w_loaded, 16)
            sp.dma_start(ac[:, :], a_cols).then_inc(w_loaded, 16)
            sp.dma_start(entT[:, :], ent_t).then_inc(entT_loaded, 16)

            def load(k, u, odd):
                if not (k == 0 and isinstance(u, int) and u < 2):
                    sp.wait_ge(walls_made, PAIRS * k + u - 1)
                w = WIDTH[k]
                src = adj_t[NJ * START[k]:NJ * (START[k] + w)].rearrange("(v p m) -> v p m", p=P, m=2 * w)
                src = src[bass.ds(u, 1)].rearrange("v p m -> (v p) m")
                sp.dma_start(adj_in[:, odd, 0:2 * w], src).then_inc(adj_loaded[odd], 16)

            load(0, 0, 0)
            load(0, 1, 1)
            sp.dma_start(xT[:, :], x_t).then_inc(xT_loaded, 16)
            load(0, 2, 0)
            load(0, 3, 1)
            sp.dma_start(xr[:, 0:TILES, :], ent_rows).then_inc(ent_loaded, 16)
            for k in range(BLOCKS + 2):
                if k < BLOCKS:
                    with sp.Fori(2 if k == 0 else 0, 3 * PAIRS // 8) as w:
                        load(k, w * 2, 0)
                        load(k, w * 2 + 1, 1)
                if k == 1:
                    sp.wait_ge(ent_made, 1)
                    sp.dma_start(xr[:, :, :], x_rows).then_inc(x_loaded, 16)
                if k >= 2:
                    b = k - 2
                    sp.wait_ge(fin, FINS * (b + 1))
                    here = slice(START[b] // P, (START[b] + WIDTH[b]) // P)
                    sp.dma_start(out[:, here, :], yout[:, 0:WIDTH[b] // P, :]).then_inc(out_stored, 16)
                if k < BLOCKS:
                    with sp.Fori(3 * PAIRS // 8, PAIRS // 2) as w:
                        load(k, w * 2, 0)
                        load(k, w * 2 + 1, 1)
            sp.wait_ge(out_stored, 16 * BLOCKS)

        @block.scalar
        def _(act):
            def step(k, u, odd=None):
                odd = u % 2 if odd is None and isinstance(u, int) else (odd or 0)
                g = PAIRS * k + u
                if 1 <= k <= BLOCKS and isinstance(u, int) and u == AHEAD + 3:
                    w = WIDTH[k - 1]
                    act.wait_ge(rows_mm, k)
                    nc.scalar.copy(row_a[:, (k - 1) % 2, 0:w], aux[:, 0:w]).then_inc(rows_made, 1)
                    nc.scalar.copy(row_b[:, (k - 1) % 2, 0:w], aux[:, IB:IB + w]).then_inc(rows_made, 1)
                if k >= 2 and isinstance(u, int):
                    b = k - 2
                    w, ch = WIDTH[b], WIDTH[b] // P
                    if u == LAG + AHEAD + 2:
                        act.wait_ge(prob_used, TILES * (b + 1))
                        if b >= 1:
                            act.wait_ge(numerT_made, b)
                        nc.scalar.copy(numer_sb[0:FE, 0:w], numer[b % 2][0:FE, 0:w]).then_inc(numer_copied, 1)
                    if u == LAG + AHEAD + 3:
                        act.wait_ge(fin, FINS * b + NEG_AT)
                        nc.scalar.activation(eneg[:, 0:ch, :], neg[:, 0:ch, :], ACT.Exp).then_inc(eneg_made, 1)
                    if u == LAG + AHEAD + 4:
                        act.wait_ge(fin, FINS * b + Y_AT)
                        nc.scalar.activation(sq[:, 0:ch, :], y[:, 0:ch, :], ACT.Square).then_inc(sq_made, 1)
                if k < BLOCKS:
                    act.wait_ge(adj_loaded[odd], 16 * (PAIRS // 2 * k + 1) + 8 * (u - odd))
                    if k >= 2 or (k == 1 and not (isinstance(u, int) and u < RING - PAIRS)):
                        act.wait_ge(masked_made, 2 * (g - RING + 1))
                    nc.scalar.activation(slot(k, u), adj_in[:, odd, 0:2 * WIDTH[k]], ACT.Relu,
                                         bias=wall_col[:, :], scale=-WALL).then_inc(walls_made, 1)
                if second(k, u, LAG + AHEAD):
                    b, v = second(k, u, LAG + AHEAD)
                    place = 2 * ((odd + LAG + AHEAD) % 2)
                    for t in range(2):
                        n = TILES * b + 2 * v + t
                        act.wait_ge(masked_made, n + 1)
                        if not (b == 0 and isinstance(v, int) and v < PR // 2):
                            act.wait_ge(prob_used, n + 1 - PR)
                        nc.scalar.activation(prob[:, place + t, 0:WIDTH[b]], masked[:, t, 0:WIDTH[b]], ACT.Exp,
                                             bias=s2_02[:, bass.ds(2 * v + t, 1)]).then_inc(prob_made, 1)
                if k == 0 and isinstance(u, int) and u == PEEL - 1:
                    act.wait_ge(s1_mm, 1)

            act.wait_ge(wall_made, 1)
            steps(act, step)

        @block.gpsimd
        def _(pool):
            nc.gpsimd.memset(ident[:, :], 0.0).then_inc(ident_zero, 1)
            pool.wait_ge(ident_zero, 1)
            nc.gpsimd.affine_select(out=ident[:, :], in_=ident[:, :], compare_op=ALU.not_equal, fill=1.0, base=0,
                                    pattern=[[-1, P]], channel_multiplier=1).then_inc(ident_made, 1)
            nc.gpsimd.memset(ent3[:, :, F:FE], 1.0).then_inc(pad_made, 1)
            nc.gpsimd.memset(half[:, :], -0.5).then_inc(half_made, 1)
            pool.wait_ge(ext_made, 2)
            nc.gpsimd.partition_all_reduce(gext[:, :], ext[:, :], P, RMAX).then_inc(gext_made, 1)
            pool.wait_ge(ent_loaded, 16)
            nc.gpsimd.tensor_copy(ent3[:, :, 0:F], xr[:, 0:TILES, :]).then_inc(ent_made, 1)

            def step(k, u, odd=None):
                odd = u % 2 if odd is None and isinstance(u, int) else (odd or 0)
                if k >= 2 and isinstance(u, int) and u == LAG:
                    b = k - 2
                    pool.wait_ge(sum_made, 1)
                    pool.wait_ge(col, COLS * (b + 1))
                    ch, c0 = WIDTH[b] // P, START[b] // P
                    nc.gpsimd.tensor_tensor(uniform[:, 0:ch, :],
                                            bare[:, c0:c0 + ch].unsqueeze(2).to_broadcast([P, ch, FE]),
                                            ent_sum[:, :].unsqueeze(1).to_broadcast([P, ch, FE]),
                                            ALU.mult).then_inc(uniform_made, 1)
                if k >= 2 and isinstance(u, int) and u == LAG + 5:
                    b = k - 2
                    pool.wait_ge(fin, FINS * b + VAR_AT)
                    ch = WIDTH[b] // P
                    nc.gpsimd.tensor_tensor(rstd[:, 0:ch], var[:, 0:ch], half[:, 0:ch], ALU.pow).then_inc(rstd_made, 1)
                if second(k, u):
                    b, v = second(k, u)
                    for t in range(2):
                        n = TILES * b + 2 * v + t
                        pool.wait_ge(z_made, n + 1)
                        if not (b == 0 and isinstance(v, int) and v == 0):
                            pool.wait_ge(prob_made, n - 1)
                        nc.gpsimd.tensor_tensor(masked[:, t, 0:WIDTH[b]], z[:, 2 * ((odd + LAG) % 2) + t, 0:WIDTH[b]],
                                                slot(b, v, t, 1),
                                                ALU.subtract).then_inc(masked_made, 1)

            steps(pool, step)

        @block.vector
        def _(dve):
            n_setup = [0]

            def link(ins):
                n_setup[0] += 1
                ins.then_inc(setup, 1)
                dve.wait_ge(setup, n_setup[0])

            nc.vector.memset(wall_col[:, :], WALL).then_inc(wall_made, 1)
            nc.vector.memset(ones[:, :], 1.0).then_inc(ones_made, 1)
            dve.wait_ge(wa_mm, 1)
            nc.vector.tensor_copy(wa[:, :], aux[:, BANK:BANK + 2]).then_inc(wa_made, 1)
            dve.wait_ge(s2_mm, 1)
            link(nc.vector.tensor_copy(s2[:, :].rearrange("p (h t) -> p h t", h=2), score_cols(0)))
            nc.vector.tensor_reduce(ext[:, 0:1], s2[:, :], AX_X, ALU.max).then_inc(ext_made, 1)
            link(nc.vector.tensor_scalar(s2_lev[:, :], s2[:, :], -1.0, None, ALU.mult))
            nc.vector.tensor_reduce(ext[:, 1:2], s2_lev[:, :], AX_X, ALU.max).then_inc(ext_made, 1)
            nc.vector.tensor_scalar(s2_08[:, :], s2[:, :], 1.0 - ALPHA, None, ALU.mult)
            link(nc.vector.tensor_scalar(s2_02[:, :], s2[:, :], ALPHA, None, ALU.mult))
            dve.wait_ge(gext_made, 1)
            link(nc.vector.tensor_tensor(sc[:, 0:1], gext[:, 0:1], gext[:, 1:2], ALU.add))
            link(nc.vector.tensor_scalar(sc[:, 1:2], sc[:, 0:1], 1e-6, 1.0 / LEVELS, ALU.max, ALU.mult))
            link(nc.vector.reciprocal(sc[:, 2:3], sc[:, 1:2]))
            link(nc.vector.tensor_scalar(s2_lev[:, :], s2[:, :], gext[:, 1:2], sc[:, 2:3], ALU.add, ALU.mult))
            link(nc.vector.tensor_scalar(s2_lev[:, :], s2_lev[:, :], 1.0, None, ALU.add))

            def top_ends(b):
                dve.wait_ge(top_made, (PAIRS - 1) * (b + 1))
                if b >= 1:
                    dve.wait_ge(rows_mm, b)
                w = WIDTH[b]
                nc.vector.tensor_tensor(topf[:, 0:w], top[:, 0, 0:w], top[:, 1, 0:w], ALU.max).then_inc(topf_made, 1)

            def columns(b):
                n = [COLS * b]

                def chain(ins):
                    n[0] += 1
                    ins.then_inc(col, 1)
                    dve.wait_ge(col, n[0])

                ch, c0 = WIDTH[b] // P, START[b] // P
                here = slice(c0, c0 + ch)
                dve.wait_ge(topT_made, b + 1)
                chain(nc.vector.tensor_reduce(q[:, 0:ch], aux[:, 0:WIDTH[b]].rearrange("p (c j) -> p c j", j=P), AX_X, ALU.max))
                chain(nc.vector.tensor_scalar(bare[:, here], q[:, 0:ch], 0.0, None, ALU.is_equal))
                chain(nc.vector.tensor_scalar(mu[:, 0:ch], q[:, 0:ch], sc[:, 1:2], gext[:, 1:2], ALU.mult, ALU.subtract))
                chain(nc.vector.tensor_tensor(sm[:, 0:ch], mu[:, 0:ch], s1[:, here], ALU.add))
                chain(nc.vector.scalar_tensor_tensor(out=mx[:, 0:ch], in0=sm[:, 0:ch], scalar=ALPHA, in1=sm[:, 0:ch],
                                                     op0=ALU.mult, op1=ALU.max))
                chain(nc.vector.tensor_tensor(col_a[:, 0:ch], s1[:, here], mx[:, 0:ch], ALU.subtract))
                chain(nc.vector.scalar_tensor_tensor(out=col_b[:, 0:ch], in0=s1[:, here], scalar=ALPHA, in1=mx[:, 0:ch],
                                                     op0=ALU.mult, op1=ALU.subtract))
                if b == 0:
                    dve.wait_ge(ident_made, 1)
                for d, c in ((diag_a, col_a), (diag_b, col_b)):
                    nc.vector.tensor_tensor(d[:, 0:ch, :], ident[:, :].unsqueeze(1).to_broadcast([P, ch, P]),
                                            c[:, 0:ch].unsqueeze(2).to_broadcast([P, ch, P]),
                                            ALU.mult).then_inc(diag_made, 1)

            def finish(b, part):
                n = [FINS * b + {0: 0, 1: NEG_AT, 2: Y_AT, 3: VAR_AT}[part]]

                def chain(ins, hold=True):
                    n[0] += 1
                    ins.then_inc(fin, 1)
                    if hold:
                        dve.wait_ge(fin, n[0])

                ch, c0 = WIDTH[b] // P, START[b] // P
                wide = [P, ch, F]
                xs = xr[:, c0:c0 + ch, :]
                if part == 0:
                    dve.wait_ge(numerT_made, b + 1)
                    dve.wait_ge(uniform_made, b + 1)
                    banks, per = ch // BC, BC * FE
                    tr = aux[:, 0:banks * BANK].rearrange("p (a r) -> p a r", r=BANK)[:, :, 0:per]
                    uni = uniform[:, 0:ch, :].rearrange("p (a c) f -> p a (c f)", a=banks)
                    chain(nc.vector.tensor_tensor(uni, tr, uni, ALU.add))
                    chain(nc.vector.reciprocal(rden[:, 0:ch].unsqueeze(2), uniform[:, 0:ch, F:F + 1]))
                    chain(nc.vector.tensor_tensor(h[:, 0:ch, :], uniform[:, 0:ch, 0:F], rden[:, 0:ch].unsqueeze(2).to_broadcast(wide),
                                                  ALU.mult))
                    if b == 0:
                        dve.wait_ge(x_loaded, 16)
                    chain(nc.vector.tensor_tensor(h[:, 0:ch, :], h[:, 0:ch, :], xs, ALU.add))
                    if b >= 1:
                        dve.wait_ge(out_stored, 16 * b)
                    chain(nc.vector.tensor_scalar(neg[:, 0:ch, :], h[:, 0:ch, :], 0.0, None, ALU.min), hold=False)
                if part == 1:
                    dve.wait_ge(eneg_made, b + 1)
                    chain(nc.vector.scalar_tensor_tensor(out=h[:, 0:ch, :], in0=h[:, 0:ch, :], scalar=0.0, in1=eneg[:, 0:ch, :],
                                                         op0=ALU.max, op1=ALU.add))
                    chain(nc.vector.scalar_tensor_tensor(out=h[:, 0:ch, :], in0=h[:, 0:ch, :], scalar=-1.0, in1=xs,
                                                         op0=ALU.add, op1=ALU.add))
                    chain(nc.vector.tensor_reduce(mean[:, 0:ch], h[:, 0:ch, :], AX_X, ALU.add))
                    chain(nc.vector.tensor_scalar(mean[:, 0:ch], mean[:, 0:ch], 1.0 / F, None, ALU.mult))
                    chain(nc.vector.tensor_tensor(y[:, 0:ch, :], h[:, 0:ch, :], mean[:, 0:ch].unsqueeze(2).to_broadcast(wide),
                                                  ALU.subtract), hold=False)
                if part == 2:
                    dve.wait_ge(sq_made, b + 1)
                    chain(nc.vector.tensor_reduce(var[:, 0:ch], sq[:, 0:ch, :], AX_X, ALU.add))
                    chain(nc.vector.tensor_scalar(var[:, 0:ch], var[:, 0:ch], 1.0 / F, EPS, ALU.mult, ALU.add), hold=False)
                if part == 3:
                    dve.wait_ge(rstd_made, b + 1)
                    chain(nc.vector.tensor_tensor(yout[:, 0:ch, :], y[:, 0:ch, :],
                                                  rstd[:, 0:ch].unsqueeze(2).to_broadcast(wide), ALU.mult), hold=False)

            def step(k, u, odd=None):
                g = PAIRS * k + u
                fixed = isinstance(u, int)
                odd = u % 2 if odd is None and fixed else (odd or 0)
                if 1 <= k <= BLOCKS and fixed and u == 0:
                    top_ends(k - 1)
                if k < BLOCKS:
                    dve.wait_ge(walls_made, g + 1)
                    first = fixed and u == 0
                    dst = top if first else level
                    if first and k >= 1:
                        dve.wait_ge(topf_made, k)
                    if not first and not (k == 0 and fixed and u == 1):
                        dve.wait_ge(top_made, (PAIRS - 1) * k + u - 1)
                    for t in range(2):
                        nc.vector.tensor_scalar(dst[:, t, 0:WIDTH[k]], slot(k, u, t, 1), 0.0, s2_lev[:, bass.ds(2 * u + t, 1)],
                                                ALU.is_equal, ALU.mult).then_inc(level_made, 1)
                sec = second(k, u)
                for t in range(2):
                    if sec:
                        b, v = sec
                        n = TILES * b + 2 * v + t
                        if fixed and v == 0 and t == 0:
                            dve.wait_ge(rows_made, 2 * (b + 1))
                        if not (b == 0 and fixed and v < ZR // 2):
                            dve.wait_ge(masked_made, n + 1 - ZR)
                        nc.vector.scalar_tensor_tensor(out=z[:, 2 * ((odd + LAG) % 2) + t, 0:WIDTH[b]],
                                                       in0=row_a[:, b % 2, 0:WIDTH[b]],
                                                       scalar=s2_08[:, bass.ds(2 * v + t, 1)], in1=row_b[:, b % 2, 0:WIDTH[b]],
                                                       op0=ALU.add, op1=ALU.max).then_inc(z_made, 1)
                    if t == 0 and k < BLOCKS and not first:
                        dve.wait_ge(level_made, 2 * (g + 1))
                        now = top[:, :, 0:WIDTH[k]]
                        nc.vector.tensor_tensor(now, now, level[:, :, 0:WIDTH[k]],
                                                ALU.max).then_inc(top_made, 1)
                if 1 <= k <= BLOCKS and fixed and u == 1:
                    columns(k - 1)
                if k >= 2 and fixed and LAG + 2 <= u <= LAG + 5:
                    finish(k - 2, u - LAG - 2)
                if k == 0 and fixed and u == PEEL - 1:
                    dve.wait_ge(s1_mm, 1)
                    link(nc.vector.tensor_copy(s1[:, :].rearrange("p (h t) -> p h t", h=2), score_cols(2)))
                    dve.wait_ge(sum_mm, 1)
                    nc.vector.tensor_copy(ent_sum[:, :], numer[1][:, 0:FE]).then_inc(sum_made, 1)

            steps(dve, step)

        @block.tensor
        def _(pe):
            pe.wait_ge(w_loaded, 32)
            nc.tensor.matmul(aux[0:F, BANK:BANK + 2], wt[:, :], ac[:, :], start=True, stop=True)
            nc.tensor.matmul(aux[F:P, BANK:BANK + 2], wt[:, :], ac[:, :], start=True, stop=True).then_inc(wa_mm, 1)
            pe.wait_ge(wa_made, 1)
            pe.wait_ge(entT_loaded, 16)
            for t in (t + h * TILES // 2 for t in range(TILES // 2) for h in range(2)):
                lo, at = F * (t // (TILES // 2)), t % (TILES // 2) * P
                mm = nc.tensor.matmul(score_col(0, t), entT[lo:lo + F, at:at + P], wa[lo:lo + F, 1:2],
                                      start=True, stop=True)
            mm.then_inc(s2_mm, 1)
            pe.wait_ge(xT_loaded, 16)
            for t in (t + h * C_ALL // 2 for t in range(C_ALL // 2) for h in range(2)):
                lo, at = F * (t // (C_ALL // 2)), t % (C_ALL // 2) * P
                mm = nc.tensor.matmul(score_col(2, t), xT[lo:lo + F, at:at + P], wa[lo:lo + F, 0:1],
                                      start=True, stop=True)
            mm.then_inc(s1_mm, 1)
            pe.wait_ge(ent_made, 1)
            pe.wait_ge(pad_made, 1)
            pe.wait_ge(ones_made, 1)
            for t in range(TILES):
                mm = nc.tensor.matmul(numer[1][:, 0:FE], ones[:, :], ent3[:, t, :],
                                      start=(t == 0), stop=(t == TILES - 1))
            mm.then_inc(sum_mm, 1)
            pe.wait_ge(ident_made, 1)

            def step(k, u, odd=None):
                fixed = isinstance(u, int)
                odd = u % 2 if odd is None and fixed else (odd or 0)
                if 1 <= k <= BLOCKS and fixed and u == 0:
                    b = k - 1
                    pe.wait_ge(topf_made, b + 1)
                    if b == 0:
                        pe.wait_ge(sum_made, 1)
                    if b >= 2:
                        pe.wait_ge(fin, FINS * (b - 2) + 1)
                    for c in range(WIDTH[b] // P):
                        mm = nc.tensor.transpose(aux[:, c * P:(c + 1) * P], topf[:, c * P:(c + 1) * P], ident[:, :])
                    mm.then_inc(topT_made, 1)
                if 1 <= k <= BLOCKS and fixed and u == 1:
                    b = k - 1
                    pe.wait_ge(diag_made, 2 * (b + 1))
                    for r, d in enumerate((diag_a, diag_b)):
                        dflat = d[:, :, :].rearrange("p c j -> p (c j)")
                        for i in range(WIDTH[b] // BANK):
                            mm = nc.tensor.matmul(aux[:, r * IB + i * BANK:r * IB + (i + 1) * BANK], ones[:, :],
                                                  dflat[:, i * BANK:(i + 1) * BANK], start=True, stop=True)
                    mm.then_inc(rows_mm, 1)
                if k >= 2 and fixed and u == LAG + 1:
                    b = k - 2
                    pe.wait_ge(numer_copied, b + 1)
                    if k <= BLOCKS:
                        pe.wait_ge(rows_made, 2 * k)
                    if b >= 1:
                        pe.wait_ge(fin, FINS * (b - 1) + 1)
                    for c in range(WIDTH[b] // P):
                        at = c // BC * BANK + c % BC * FE
                        mm = nc.tensor.transpose(aux[:, at:at + FE], numer_sb[0:FE, c * P:(c + 1) * P],
                                                 ident[0:FE, 0:FE])
                    mm.then_inc(numerT_made, 1)
                if second(k, u):
                    b, v = second(k, u)
                    first = fixed and v == 0
                    last = fixed and v == PAIRS - 1
                    for t in range(2):
                        pe.wait_ge(prob_made, TILES * b + 2 * v + t + 1)
                        if first and t == 0 and b >= 2:
                            pe.wait_ge(numer_copied, b - 1)
                        for i in range(WIDTH[b] // BANK):
                            mm = nc.tensor.matmul(numer[b % 2][0:FE, i * BANK:(i + 1) * BANK],
                                                  ent[:, bass.ds((2 * v + t) * FE, FE)],
                                                  prob[:, 2 * ((odd + LAG) % 2) + t, i * BANK:(i + 1) * BANK],
                                                  start=first and t == 0, stop=last and t == 1)
                        mm.then_inc(prob_used, 1)

            for k in range(BLOCKS + 2):
                for u in range(PAIRS if k <= BLOCKS else PEEL):
                    step(k, u)


def kernel(x, adj, L0_gnn_entity_embs, L0_gnn_W, L0_gnn_a):
    import numpy as np
    import concourse.bacc as bacc
    from concourse.bass_utils import run_bass_kernel_spmd

    x, adj, ent, w, a = (np.asarray(v) for v in (x, adj, L0_gnn_entity_embs, L0_gnn_W, L0_gnn_a))
    n_i, n_j = adj.shape
    f = w.shape[1]
    pairs = n_j // 256
    cut = [sum(WIDTHS[:b]) for b in range(len(WIDTHS) + 1)]
    assert cut[-1] == n_i
    arrays = {
        "adj_t": np.concatenate([adj[lo:hi].reshape(hi - lo, pairs, 2, 128).transpose(1, 3, 2, 0).reshape(-1)
                                 for lo, hi in zip(cut, cut[1:])]),
        "x_t": x.reshape(2, n_i // 2, f).transpose(0, 2, 1).reshape(2 * f, n_i // 2),
        "x_rows": x.reshape(n_i // 128, 128, f).transpose(1, 0, 2),
        "ent_t": ent.reshape(2, n_j // 2, f).transpose(0, 2, 1).reshape(2 * f, n_j // 2),
        "ent_rows": ent.reshape(n_j // 128, 128, f).transpose(1, 0, 2),
        "w_t": w.T,
        "a_cols": a.reshape(2, f).T,
    }
    arrays = {k: np.ascontiguousarray(v) for k, v in arrays.items()}
    nc = bacc.Bacc("TRN2", target_bir_lowering=False, num_devices=1)
    args = {k: nc.dram_tensor(k, v.shape, mybir.dt.from_np(v.dtype), kind="ExternalInput").ap()
            for k, v in arrays.items()}
    out = nc.dram_tensor("out", (128, n_i // 128, f), F32, kind="ExternalOutput").ap()
    gat_layernorm(nc, out=out, **args)
    r = run_bass_kernel_spmd(nc, [arrays], core_ids=[0])
    return r.results[0]["out"].transpose(1, 0, 2).reshape(n_i, f)
```

```python
from contextlib import ExitStack

import concourse.bass as bass
from concourse import mybir

ALU = mybir.AluOpType
ACT = mybir.ActivationFunctionType
BF16 = mybir.dt.bfloat16
F32 = mybir.dt.float32
I32 = mybir.dt.int32
U16 = mybir.dt.uint16
AX_X = mybir.AxisListType.X
RMAX = bass.bass_isa.ReduceOp.max

P = 128
ALPHA = 0.2
EPS = 1e-5
WALL = 2.0 ** 90
LEVELS = 65000.0
WIDTHS = (512, 1024, 1024, 1024, 512)


def gat_layernorm(nc: bass.Bass, adj_t, x_rows, ent_rows, w_t, a_cols, out):
    F = w_t.shape[0]
    NJ, NI = P * ent_rows.shape[1], P * x_rows.shape[1]
    WIDTH = WIDTHS
    BLOCKS, WIDEST = len(WIDTH), max(WIDTH)
    START = [sum(WIDTH[:b]) for b in range(BLOCKS)]
    TILES = NJ // P
    PAIRS, QUADS = TILES // 2, TILES // 4
    TOTAL = TILES * BLOCKS
    CHUNKS, ALL_CHUNKS = WIDEST // P, NI // P
    F_ONES = F + 2
    BANK_COLS = 512
    CHUNKS_PER_BANK = 4
    AHEAD = 2
    LAG = 3
    RING = PAIRS + LAG + AHEAD + 1
    PEEL = LAG + 9
    NUMER_LAG = 4
    Z_PLACES, PROB_PLACES = 4, 4
    HALVED = BLOCKS - 2
    COLS, FINS = 8, 13
    NEG_AT, ELU_AT, Y_AT, VAR_AT = 5, 7, 10, 12

    with ExitStack() as ctx:
        def sb(name, shape, dt):
            return ctx.enter_context(nc.sbuf_tensor(name, shape, dt))

        def sem(name):
            return ctx.enter_context(nc.semaphore(name))

        aux = ctx.enter_context(nc.psum_tensor("aux", [P, WIDEST], F32))
        shift = ctx.enter_context(nc.psum_tensor("shift", [P, 2, WIDEST], F32))
        numer = ctx.enter_context(nc.psum_tensor("numer", [P, WIDEST], F32))

        adj_in = sb("adj_in", [P, 2, 2 * WIDEST], I32)
        walls = sb("walls", [P, RING * 2 * WIDEST], BF16)
        level = sb("level", [P, 2, WIDEST], U16)
        top = sb("top", [P, 2, WIDEST], U16)
        top_f32 = sb("top_f32", [P, WIDEST], F32)
        s1_row = sb("s1_row", [P, NI], F32)
        shift_all = sb("shift_all", [P, 2, WIDEST], F32)
        shift_rows = sb("shift_rows", [2, 2, WIDEST], BF16)
        z = sb("z", [P, Z_PLACES, WIDEST], F32)
        prob = sb("prob", [P, PROB_PLACES, WIDEST], F32)
        ent = sb("ent", [P, TILES * F_ONES], F32)
        ent_ones = ent[:, :].rearrange("p (t f) -> p t f", f=F_ONES)
        x_in = sb("x_in", [P, ALL_CHUNKS, F], F32)
        numer_out = top_f32
        ident = sb("ident", [P, P], F32)
        ones = sb("ones", [P, P], F32)
        ident_bf = sb("ident_bf", [P, P], BF16)
        minus_ident = sb("minus_ident", [P, P], BF16)
        ones_bf = sb("ones_bf", [2, P], BF16)
        w_in = sb("w_in", [F, F], F32)
        a_in = sb("a_in", [F, 2], F32)
        wa = sb("wa", [P, 2, F], F32)
        s2 = sb("s2", [P, TILES], F32)
        s2_minus = sb("s2_minus", [P, TILES], F32)
        s2_lev = sb("s2_lev", [P, TILES], F32)
        s1 = sb("s1", [P, ALL_CHUNKS], F32)
        s1_scaled = sb("s1_scaled", [P, ALL_CHUNKS], F32)
        extremes = sb("extremes", [P, 2], F32)
        all_extremes = sb("all_extremes", [P, 2], F32)
        scales = sb("scales", [P, 3], F32)
        top_level = sb("top_level", [P, CHUNKS], F32)
        top_s2 = sb("top_s2", [P, CHUNKS], F32)
        top_sum = sb("top_sum", [P, CHUNKS], F32)
        top_score = sb("top_score", [P, CHUNKS], F32)
        parts = sb("parts", [P, CHUNKS, 2], BF16)
        shift_col = sb("shift_col", [P, CHUNKS], F32)
        bare = sb("bare", [P, ALL_CHUNKS], F32)
        ent_sum = sb("ent_sum", [P, F_ONES], F32)
        uniform = sb("uniform", [P, CHUNKS, F_ONES], F32)
        rden = sb("rden", [P, CHUNKS], F32)
        h = sb("h", [P, CHUNKS, F], F32)
        neg = sb("neg", [P, CHUNKS, F], F32)
        y = sb("y", [P, CHUNKS, F], F32)
        eneg = sq = yout = neg
        mean = sb("mean", [P, CHUNKS], F32)
        var = sb("var", [P, CHUNKS], F32)
        rstd = sb("rstd", [P, CHUNKS], F32)
        wall_col = sb("wall_col", [P, 1], F32)
        minus_half = sb("minus_half", [P, CHUNKS], F32)

        ent_in = prob[:, 0:2, :].rearrange("p t i -> p (t i)")[:, 0:TILES * F].rearrange("p (t f) -> p t f", f=F)
        ent_wa = z[:, 0:2, :].rearrange("p t i -> p (t i)")[:, 0:TILES * F].rearrange("p (t f) -> p t f", f=F)
        x_wa = prob[:, 2:4, :].rearrange("p t i -> p (t i)")[:, 0:ALL_CHUNKS * F].rearrange("p (t f) -> p t f", f=F)

        adj_loaded = [sem(f"adj_loaded{i}") for i in range(2)]
        early_loaded = [sem(f"early_loaded{i}") for i in range(4)]
        w_loaded = sem("w_loaded")
        ent_loaded = sem("ent_loaded")
        ent_made = sem("ent_made")
        x_wa_made = sem("x_wa_made")
        s1_made = sem("s1_made")
        s1_mm = sem("s1_mm")
        s1_row_made = sem("s1_row_made")
        bf16_made = sem("bf16_made")
        x_loaded = sem("x_loaded")
        out_stored = sem("out_stored")
        ones_made = sem("ones_made")
        ident_zero = sem("ident_zero")
        ident_made = sem("ident_made")
        pad_made = sem("pad_made")
        wall_made = sem("wall_made")
        minus_half_made = sem("minus_half_made")
        wa_mm = sem("wa_mm")
        wa_made = sem("wa_made")
        sum_mm = sem("sum_mm")
        setup_made = sem("setup_made")
        extremes_made = sem("extremes_made")
        all_extremes_made = sem("all_extremes_made")
        sum_made = sem("sum_made")
        walls_made = sem("walls_made")
        level_made = sem("level_made")
        top_made = sem("top_made")
        z_made = sem("z_made")
        shift_made = sem("shift_made")
        spread_mm = sem("spread_mm")
        spread_made = sem("spread_made")
        open_made = sem("open_made")
        walled_made = sem("walled_made")
        prob_made = sem("prob_made")
        prob_used = sem("prob_used")
        top_f32_made = sem("top_f32_made")
        top_turned = sem("top_turned")
        cols_made = sem("cols_made")
        rows_mm = sem("rows_mm")
        rows_made = sem("rows_made")
        numer_copied = sem("numer_copied")
        numer_turned = sem("numer_turned")
        uniform_made = sem("uniform_made")
        fin_made = sem("fin_made")
        eneg_made = sem("eneg_made")
        sq_made = sem("sq_made")
        rstd_made = sem("rstd_made")

        def early_in(u):
            return adj_in[:, u // 2 % 2, u % 2 * WIDEST:u % 2 * WIDEST + 2 * WIDTH[0]]

        def slot(b, v, t=0, n=2):
            s = ((PAIRS * b + v) % RING) * (2 * WIDEST)
            return walls[:, bass.ds(s + t * WIDTH[b], n * WIDTH[b])]

        def owned(b, t, par):
            return t == 1 and (b >= HALVED or (b >= 1 and par == 1))

        def place_of(b, t, par):
            return par if b >= HALVED else t

        def count(b, v, t, par):
            twos = (v - par) // 2
            if owned(b, t, par):
                return (b - 1) * QUADS + twos + 1 if b < HALVED else (HALVED - 1) * QUADS + (b - HALVED) * PAIRS + v + 1
            if b == 0:
                return 2 * v + t + 1
            if b < HALVED:
                return TILES + (b - 1) * 3 * QUADS + 3 * twos + 2 * par + t + 1
            return TILES + (HALVED - 1) * 3 * QUADS + (b - HALVED) * PAIRS + v + 1

        def steps(eng, do):
            for k in range(BLOCKS + 2):
                for u in range(PEEL if k else PAIRS):
                    do(k, u)
                if 1 <= k <= BLOCKS:
                    with eng.Fori(PEEL // 2, PAIRS // 2) as w:
                        do(k, w * 2)
                        do(k, w * 2 + 1, 1)

        def second(k, u, lag=LAG):
            early = isinstance(u, int) and u < lag
            b, v = (k - 2, u + PAIRS - lag) if early else (k - 1, u - lag)
            return (b, v) if 0 <= b < BLOCKS else None

        block = ctx.enter_context(nc.Block())

        @block.sync
        def _(sp):
            sp.dma_start(w_in[:, :], w_t).then_inc(w_loaded, 16)
            sp.dma_start(a_in[:, :], a_cols).then_inc(w_loaded, 16)
            sp.dma_start(ent_in, ent_rows).then_inc(ent_loaded, 16)

            def load(k, u, odd):
                sp.wait_ge(walls_made, PAIRS * k + u - 1)
                w = WIDTH[k]
                src = adj_t[NJ * START[k]:NJ * (START[k] + w)].rearrange("(v p m) -> v p m", p=P, m=2 * w)
                src = src[bass.ds(u, 1)].rearrange("v p m -> (v p) m")
                sp.dma_start(adj_in[:, odd, 0:2 * w], src).then_inc(adj_loaded[odd], 16)

            def load_early(u):
                if u >= 4:
                    sp.wait_ge(walls_made, u - 3)
                m = 2 * WIDTH[0]
                src = adj_t[P * m * u:P * m * (u + 1)].rearrange("(p m) -> p m", p=P)
                sp.dma_start(early_in(u), src).then_inc(early_loaded[u % 4], 16)

            for u in range(PAIRS):
                load_early(u)
                if u == 7:
                    sp.dma_start(x_in[:, :, :], x_rows).then_inc(x_loaded, 16)
            for k in range(1, BLOCKS + 2):
                if k < BLOCKS:
                    with sp.Fori(0, 7 * PAIRS // 16) as w:
                        load(k, w * 2, 0)
                        load(k, w * 2 + 1, 1)
                if k >= 2:
                    b = k - 2
                    sp.wait_ge(fin_made, FINS * (b + 1))
                    here = slice(START[b] // P, (START[b] + WIDTH[b]) // P)
                    sp.dma_start(out[:, here, :], yout[:, 0:WIDTH[b] // P, :]).then_inc(out_stored, 16)
                if k < BLOCKS:
                    with sp.Fori(7 * PAIRS // 16, PAIRS // 2) as w:
                        load(k, w * 2, 0)
                        load(k, w * 2 + 1, 1)
            sp.wait_ge(out_stored, 16 * BLOCKS)

        @block.scalar
        def _(act):
            def step(k, u, odd=None):
                odd = u % 2 if odd is None and isinstance(u, int) else (odd or 0)
                g = PAIRS * k + u
                if 1 <= k <= BLOCKS and isinstance(u, int) and u == 0:
                    w, i0 = WIDTH[k - 1], START[k - 1]
                    act.wait_ge(s1_mm, k)
                    nc.scalar.copy(s1_row[:, i0:i0 + w], aux[:, 0:w]).then_inc(s1_row_made, 1)
                if 1 <= k <= BLOCKS and isinstance(u, int) and u == (AHEAD if k == 1 else AHEAD + 2):
                    w = WIDTH[k - 1]
                    act.wait_ge(rows_mm, k)
                    nc.scalar.copy(shift_rows[:, (k - 1) % 2, 0:w], aux[0:2, 0:w]).then_inc(rows_made, 1)
                if 2 <= k <= BLOCKS and isinstance(u, int) and u == LAG + AHEAD:
                    w = WIDTH[k - 1]
                    act.wait_ge(spread_mm, k - 1)
                    nc.scalar.copy(shift_all[:, (k - 1) % 2, 0:w], aux[:, 0:w]).then_inc(spread_made, 1)
                if k >= 2 and isinstance(u, int):
                    b = k - 2
                    w, ch = WIDTH[b], WIDTH[b] // P
                    if u == LAG + AHEAD + 1:
                        act.wait_ge(prob_used, TILES * (b + 1))
                        if b >= 1:
                            act.wait_ge(numer_turned, b)
                        nc.scalar.copy(numer_out[0:F_ONES, 0:w], numer[0:F_ONES, 0:w]).then_inc(numer_copied, 1)
                    if u == LAG + AHEAD + 4:
                        act.wait_ge(fin_made, FINS * b + NEG_AT)
                        nc.scalar.activation(eneg[:, 0:ch, :], neg[:, 0:ch, :], ACT.Exp).then_inc(eneg_made, 1)
                    if u == LAG + AHEAD + 6:
                        act.wait_ge(fin_made, FINS * b + Y_AT)
                        nc.scalar.activation(sq[:, 0:ch, :], y[:, 0:ch, :], ACT.Square).then_inc(sq_made, 1)
                if k < BLOCKS:
                    if k == 0:
                        act.wait_ge(early_loaded[u % 4], 16 * (u // 4 + 1))
                        src = early_in(u)
                    else:
                        act.wait_ge(adj_loaded[odd], 16 * (PAIRS // 2 * (k - 1) + 1) + 8 * (u - odd))
                        src = adj_in[:, odd, 0:2 * WIDTH[k]]
                    nc.scalar.activation(slot(k, u), src, ACT.Relu,
                                         bias=wall_col[:, :], scale=-WALL).then_inc(walls_made, 1)
                if second(k, u, LAG + AHEAD):
                    b, v = second(k, u, LAG + AHEAD)
                    place = 2 * ((odd + LAG + AHEAD) % 2)
                    for t in range(2):
                        n = TILES * b + 2 * v + t
                        par = (odd + LAG + AHEAD) % 2
                        act.wait_ge(walled_made if owned(b, t, par) else z_made, count(b, v, t, par))
                        if b == 0 and isinstance(v, int) and v == 0:
                            act.wait_ge(ent_made, 1)
                        if b == 0 and isinstance(v, int) and v == 1:
                            act.wait_ge(s1_made, 1)
                        if not (b == 0 and isinstance(v, int) and v < PROB_PLACES // 2):
                            act.wait_ge(prob_used, n + 1 - PROB_PLACES)
                        nc.scalar.activation(prob[:, place + t, 0:WIDTH[b]], z[:, place + t, 0:WIDTH[b]], ACT.Exp,
                                             bias=s2[:, bass.ds(2 * v + t, 1)]).then_inc(prob_made, 1)

            act.wait_ge(wall_made, 1)
            steps(act, step)

        @block.gpsimd
        def _(pool):
            nc.gpsimd.memset(ident[:, :], 0.0).then_inc(ident_zero, 1)
            pool.wait_ge(ident_zero, 1)
            nc.gpsimd.affine_select(out=ident[:, :], in_=ident[:, :], compare_op=ALU.not_equal, fill=1.0, base=0,
                                    pattern=[[-1, P]], channel_multiplier=1).then_inc(ident_made, 1)
            pool.wait_ge(ident_made, 1)
            nc.gpsimd.tensor_copy(ident_bf[:, :], ident[:, :]).then_inc(bf16_made, 1)
            nc.gpsimd.memset(ones_bf[:, :], 1.0).then_inc(bf16_made, 1)
            nc.gpsimd.tensor_scalar(minus_ident[:, :], ident[:, :], -1.0, None, ALU.mult).then_inc(bf16_made, 1)
            nc.gpsimd.memset(ent_ones[:, :, F:F_ONES], 1.0).then_inc(pad_made, 1)
            nc.gpsimd.memset(minus_half[:, :], -0.5).then_inc(minus_half_made, 1)
            pool.wait_ge(extremes_made, 2)
            nc.gpsimd.partition_all_reduce(all_extremes[:, :], extremes[:, :], P, RMAX).then_inc(all_extremes_made, 1)
            nc.gpsimd.tensor_copy(ent_ones[:, :, 0:F], ent_in).then_inc(ent_made, 1)
            pool.wait_ge(x_loaded, 16)
            nc.gpsimd.tensor_tensor(x_wa, x_in[:, :, :], wa[:, 0, :].unsqueeze(1).to_broadcast([P, ALL_CHUNKS, F]),
                                    ALU.mult).then_inc(x_wa_made, 1)

            def step(k, u, odd=None):
                odd = u % 2 if odd is None and isinstance(u, int) else (odd or 0)
                if k >= 2 and isinstance(u, int) and u == LAG:
                    b = k - 2
                    pool.wait_ge(sum_made, 1)
                    pool.wait_ge(cols_made, COLS * (b + 1))
                    ch, c0 = WIDTH[b] // P, START[b] // P
                    nc.gpsimd.tensor_tensor(uniform[:, 0:ch, :],
                                            bare[:, c0:c0 + ch].unsqueeze(2).to_broadcast([P, ch, F_ONES]),
                                            ent_sum[:, :].unsqueeze(1).to_broadcast([P, ch, F_ONES]),
                                            ALU.mult).then_inc(uniform_made, 1)
                if k >= 2 and isinstance(u, int) and u == LAG + 7:
                    b = k - 2
                    pool.wait_ge(fin_made, FINS * b + VAR_AT)
                    ch = WIDTH[b] // P
                    nc.gpsimd.tensor_tensor(rstd[:, 0:ch], var[:, 0:ch], minus_half[:, 0:ch],
                                            ALU.pow).then_inc(rstd_made, 1)
                if second(k, u):
                    b, v = second(k, u)
                    par = (odd + LAG) % 2
                    if owned(b, 1, par):
                        zt = z[:, 2 * par + 1, 0:WIDTH[b]]
                        pool.wait_ge(open_made, count(b, v, 1, par))
                        nc.gpsimd.tensor_tensor(zt, zt, slot(b, v, 1, 1), ALU.subtract).then_inc(walled_made, 1)

            steps(pool, step)

        @block.vector
        def _(dve):
            n_setup = [0]

            def link(ins):
                n_setup[0] += 1
                ins.then_inc(setup_made, 1)
                dve.wait_ge(setup_made, n_setup[0])

            nc.vector.memset(wall_col[:, :], WALL).then_inc(wall_made, 1)
            nc.vector.memset(ones[:, :], 1.0).then_inc(ones_made, 1)
            dve.wait_ge(wa_mm, 1)
            nc.vector.tensor_copy(wa[:, :, :].rearrange("p s f -> p (s f)"), aux[:, 0:2 * F]).then_inc(wa_made, 1)
            dve.wait_ge(ent_loaded, 16)
            dve.wait_ge(wa_made, 1)
            link(nc.vector.tensor_tensor(ent_wa, ent_in, wa[:, 1, :].unsqueeze(1).to_broadcast([P, TILES, F]),
                                         ALU.mult))
            link(nc.vector.tensor_reduce(s2[:, :], ent_wa, AX_X, ALU.add))
            nc.vector.tensor_reduce(extremes[:, 0:1], s2[:, :], AX_X, ALU.max).then_inc(extremes_made, 1)
            link(nc.vector.tensor_scalar(s2_lev[:, :], s2[:, :], -1.0, None, ALU.mult))
            nc.vector.tensor_reduce(extremes[:, 1:2], s2_lev[:, :], AX_X, ALU.max).then_inc(extremes_made, 1)
            link(nc.vector.tensor_scalar(s2_minus[:, :], s2[:, :], -(1.0 - ALPHA), None, ALU.mult))
            dve.wait_ge(all_extremes_made, 1)
            link(nc.vector.tensor_tensor(scales[:, 0:1], all_extremes[:, 0:1], all_extremes[:, 1:2], ALU.add))
            link(nc.vector.tensor_scalar(scales[:, 1:2], scales[:, 0:1], 1e-6, 1.0 / LEVELS, ALU.max, ALU.mult))
            link(nc.vector.reciprocal(scales[:, 2:3], scales[:, 1:2]))
            link(nc.vector.tensor_scalar(s2_lev[:, :], s2[:, :], all_extremes[:, 1:2], scales[:, 2:3], ALU.add,
                                         ALU.mult))
            link(nc.vector.tensor_scalar(s2_lev[:, :], s2_lev[:, :], 1.0, None, ALU.add))

            def tops(b):
                return QUADS + (PAIRS - 1) * b

            def top_of_four(n):
                dve.wait_ge(walls_made, 2 * (n + 1))
                if n >= 2:
                    dve.wait_ge(top_made, n - 1)
                dst = (level if n else top)[:, :, :].rearrange("p a i -> p (a i)")
                w = WIDTH[0]
                for t in range(4):
                    nc.vector.tensor_scalar(dst[:, t * w:(t + 1) * w], slot(0, 2 * n + t // 2, t % 2, 1), 0.0,
                                            s2_lev[:, 4 * n + t:4 * n + t + 1], ALU.is_equal,
                                            ALU.mult).then_inc(level_made, 1)
                if n:
                    dve.wait_ge(level_made, 4 * (n + 1))
                    nc.vector.tensor_tensor(top[:, :, :], top[:, :, :], level[:, :, :], ALU.max).then_inc(top_made, 1)

            def top_ends(b):
                dve.wait_ge(top_made, tops(b) - (b == 0))
                if b >= 1:
                    dve.wait_ge(top_turned, b)
                w = WIDTH[b]
                if b == 0:
                    halves = top[:, :, 0:w]
                    nc.vector.tensor_tensor(halves, halves, top[:, :, w:2 * w], ALU.max).then_inc(top_made, 1)
                    dve.wait_ge(top_made, QUADS)
                nc.vector.tensor_tensor(top_f32[:, 0:w], top[:, 0, 0:w], top[:, 1, 0:w],
                                        ALU.max).then_inc(top_f32_made, 1)

            def columns(b):
                n = [COLS * b]

                def chain(ins):
                    n[0] += 1
                    ins.then_inc(cols_made, 1)
                    dve.wait_ge(cols_made, n[0])

                ch, c0 = WIDTH[b] // P, START[b] // P
                here = slice(c0, c0 + ch)
                dve.wait_ge(top_turned, b + 1)
                if b == 0:
                    dve.wait_ge(s1_made, 1)
                else:
                    dve.wait_ge(rows_mm, b)
                turned = aux[:, 0:WIDTH[b]].rearrange("p (c j) -> p c j", j=P)
                chain(nc.vector.tensor_reduce(top_level[:, 0:ch], turned, AX_X, ALU.max))
                chain(nc.vector.tensor_scalar(bare[:, here], top_level[:, 0:ch], 0.0, None, ALU.is_equal))
                chain(nc.vector.tensor_scalar(top_s2[:, 0:ch], top_level[:, 0:ch], scales[:, 1:2],
                                              all_extremes[:, 1:2], ALU.mult, ALU.subtract))
                chain(nc.vector.tensor_tensor(top_sum[:, 0:ch], top_s2[:, 0:ch], s1[:, here], ALU.add))
                chain(nc.vector.scalar_tensor_tensor(out=top_score[:, 0:ch], in0=top_sum[:, 0:ch], scalar=ALPHA,
                                                     in1=top_sum[:, 0:ch],
                                                     op0=ALU.mult, op1=ALU.max))
                chain(nc.vector.scalar_tensor_tensor(out=shift_col[:, 0:ch], in0=s1[:, here], scalar=ALPHA,
                                                     in1=top_score[:, 0:ch],
                                                     op0=ALU.mult, op1=ALU.subtract))
                chain(nc.vector.tensor_copy(parts[:, 0:ch, 0], shift_col[:, 0:ch]))
                chain(nc.vector.tensor_tensor(parts[:, 0:ch, 1], shift_col[:, 0:ch], parts[:, 0:ch, 0], ALU.subtract))

            def finish(b, part):
                n = [FINS * b + (0, NEG_AT, ELU_AT, Y_AT, VAR_AT)[part]]

                def chain(ins, hold=True):
                    n[0] += 1
                    ins.then_inc(fin_made, 1)
                    if hold:
                        dve.wait_ge(fin_made, n[0])

                ch, c0 = WIDTH[b] // P, START[b] // P
                wide = [P, ch, F]
                xs = x_in[:, c0:c0 + ch, :]
                if part == 0:
                    dve.wait_ge(numer_turned, b + 1)
                    dve.wait_ge(uniform_made, b + 1)
                    banks, per = ch // CHUNKS_PER_BANK, CHUNKS_PER_BANK * F_ONES
                    tr = aux[:, 0:banks * BANK_COLS].rearrange("p (a r) -> p a r", r=BANK_COLS)[:, :, 0:per]
                    uni = uniform[:, 0:ch, :].rearrange("p (a c) f -> p a (c f)", a=banks)
                    chain(nc.vector.tensor_tensor(uni, tr, uni, ALU.add))
                    chain(nc.vector.reciprocal(rden[:, 0:ch].unsqueeze(2), uniform[:, 0:ch, F:F + 1]))
                    chain(nc.vector.tensor_tensor(h[:, 0:ch, :], uniform[:, 0:ch, 0:F],
                                                  rden[:, 0:ch].unsqueeze(2).to_broadcast(wide),
                                                  ALU.mult))
                    chain(nc.vector.tensor_tensor(h[:, 0:ch, :], h[:, 0:ch, :], xs, ALU.add))
                    if b >= 1:
                        dve.wait_ge(out_stored, 16 * b)
                    chain(nc.vector.tensor_scalar(neg[:, 0:ch, :], h[:, 0:ch, :], 0.0, None, ALU.min), hold=False)
                if part == 1:
                    dve.wait_ge(eneg_made, b + 1)
                    chain(nc.vector.scalar_tensor_tensor(out=h[:, 0:ch, :], in0=h[:, 0:ch, :], scalar=0.0,
                                                         in1=eneg[:, 0:ch, :],
                                                         op0=ALU.max, op1=ALU.add))
                    chain(nc.vector.scalar_tensor_tensor(out=h[:, 0:ch, :], in0=h[:, 0:ch, :], scalar=-1.0, in1=xs,
                                                         op0=ALU.add, op1=ALU.add))
                if part == 2:
                    chain(nc.vector.tensor_reduce(mean[:, 0:ch], h[:, 0:ch, :], AX_X, ALU.add))
                    chain(nc.vector.tensor_scalar(mean[:, 0:ch], mean[:, 0:ch], 1.0 / F, None, ALU.mult))
                    chain(nc.vector.tensor_tensor(y[:, 0:ch, :], h[:, 0:ch, :],
                                                  mean[:, 0:ch].unsqueeze(2).to_broadcast(wide),
                                                  ALU.subtract), hold=False)
                if part == 3:
                    dve.wait_ge(sq_made, b + 1)
                    chain(nc.vector.tensor_reduce(var[:, 0:ch], sq[:, 0:ch, :], AX_X, ALU.add))
                    chain(nc.vector.tensor_scalar(var[:, 0:ch], var[:, 0:ch], 1.0 / F, EPS, ALU.mult, ALU.add),
                          hold=False)
                if part == 4:
                    dve.wait_ge(rstd_made, b + 1)
                    chain(nc.vector.tensor_tensor(yout[:, 0:ch, :], y[:, 0:ch, :],
                                                  rstd[:, 0:ch].unsqueeze(2).to_broadcast(wide), ALU.mult), hold=False)

            def step(k, u, odd=None):
                g = PAIRS * k + u
                fixed = isinstance(u, int)
                odd = u % 2 if odd is None and fixed else (odd or 0)
                if 1 <= k <= BLOCKS and fixed and u == 0:
                    top_ends(k - 1)
                if k == 0 and u % 2 == 0:
                    top_of_four(u // 2)
                if 1 <= k < BLOCKS:
                    dve.wait_ge(walls_made, g + 1)
                    first = fixed and u == 0
                    dst = top if first else level
                    if first:
                        dve.wait_ge(top_f32_made, k)
                    else:
                        dve.wait_ge(top_made, tops(k - 1) + u - 1)
                    for t in range(2):
                        nc.vector.tensor_scalar(dst[:, t, 0:WIDTH[k]], slot(k, u, t, 1), 0.0,
                                                s2_lev[:, bass.ds(2 * u + t, 1)],
                                                ALU.is_equal, ALU.mult).then_inc(level_made, 1)
                sec = second(k, u)
                for t in range(2):
                    if sec:
                        b, v = sec
                        n = TILES * b + 2 * v + t
                        par = (odd + LAG) % 2
                        if not (b == 0 and fixed and v < 2):
                            dve.wait_ge(prob_made, n + 1 - Z_PLACES)
                        zt = z[:, 2 * par + t, 0:WIDTH[b]]
                        s1_part = s1_row[:, START[b]:START[b] + WIDTH[b]]
                        minus = s2_minus[:, bass.ds(2 * v + t, 1)]
                        if owned(b, t, par):
                            if fixed and v == (0 if b >= HALVED else 1):
                                dve.wait_ge(spread_made, b)
                            nc.vector.scalar_tensor_tensor(out=zt, in0=s1_part, scalar=minus,
                                                           in1=shift_all[:, b % 2, 0:WIDTH[b]],
                                                           op0=ALU.max, op1=ALU.add).then_inc(open_made, 1)
                        else:
                            dve.wait_ge(shift_made, count(b, v, t, par))
                            nc.vector.scalar_tensor_tensor(out=zt, in0=s1_part, scalar=minus,
                                                           in1=shift[:, place_of(b, t, par), 0:WIDTH[b]],
                                                           op0=ALU.max, op1=ALU.add).then_inc(z_made, 1)
                    if k >= 2 and fixed and u == LAG + 5 and t == 0:
                        finish(k - 2, 2)
                    if t == 0 and 1 <= k < BLOCKS and not first:
                        dve.wait_ge(level_made, 2 * (g + 1))
                        now = top[:, :, 0:WIDTH[k]]
                        nc.vector.tensor_tensor(now, now, level[:, :, 0:WIDTH[k]],
                                                ALU.max).then_inc(top_made, 1)
                if 1 <= k <= BLOCKS and fixed and u == 0:
                    columns(k - 1)
                if k >= 2 and fixed and LAG + 3 <= u <= LAG + 7 and u != LAG + 5:
                    finish(k - 2, u - LAG - 3)
                if k == 0 and fixed and u == PEEL - 1:
                    dve.wait_ge(x_wa_made, 1)
                    nc.vector.tensor_reduce(s1[:, :], x_wa, AX_X, ALU.add).then_inc(s1_made, 1)
                    dve.wait_ge(s1_made, 1)
                    nc.vector.tensor_scalar(s1_scaled[:, :], s1[:, :], 1.0 - ALPHA, None, ALU.mult).then_inc(s1_made, 1)
                    dve.wait_ge(sum_mm, 1)
                    nc.vector.tensor_copy(ent_sum[:, :], numer[:, 0:F_ONES]).then_inc(sum_made, 1)

            steps(dve, step)

        @block.tensor
        def _(pe):
            pe.wait_ge(w_loaded, 32)
            for n in range(2):
                mm = nc.tensor.matmul(aux[:, n * F:(n + 1) * F], a_in[:, n:n + 1].to_broadcast([F, P]), w_in[:, :],
                                      start=True, stop=True)
            mm.then_inc(wa_mm, 1)
            pe.wait_ge(ent_made, 1)
            pe.wait_ge(pad_made, 1)
            pe.wait_ge(ones_made, 1)
            for t in range(TILES):
                mm = nc.tensor.matmul(numer[:, 0:F_ONES], ones[:, :], ent_ones[:, t, :],
                                      start=(t == 0), stop=(t == TILES - 1))
            mm.then_inc(sum_mm, 1)
            pe.wait_ge(ident_made, 1)
            pe.wait_ge(bf16_made, 3)

            used_at = {}

            def shift_less_wall(n):
                b, t = n // TILES, n % 2
                par = n % 4 // 2
                if n % TILES == 0:
                    pe.wait_ge(rows_made, b + 1)
                if owned(b, t, par):
                    return
                place = place_of(b, t, par)
                if place in used_at:
                    pe.wait_ge(z_made, used_at[place])
                used_at[place] = count(b, n % TILES // 2, t, par)
                wall = slot(b, n % TILES // 2, t, 1)
                for i in range(0, WIDTH[b], BANK_COLS):
                    nc.tensor.matmul(shift[:, place, i:i + BANK_COLS], minus_ident[:, :], wall[:, i:i + BANK_COLS],
                                     start=True, stop=False)
                for i in range(0, WIDTH[b], BANK_COLS):
                    mm = nc.tensor.matmul(shift[:, place, i:i + BANK_COLS], ones_bf[:, :],
                                          shift_rows[:, b % 2, i:i + BANK_COLS],
                                          start=False, stop=True)
                mm.then_inc(shift_made, 1)

            def sums(n):
                b, j = n // TILES, n % TILES
                pe.wait_ge(prob_made, n + 1)
                if n == 0:
                    pe.wait_ge(sum_made, 1)
                if j == 0 and b >= 1:
                    pe.wait_ge(numer_copied, b)
                for i in range(0, WIDTH[b], BANK_COLS):
                    mm = nc.tensor.matmul(numer[0:F_ONES, i:i + BANK_COLS], ent_ones[:, j, :],
                                          prob[:, n % PROB_PLACES, i:i + BANK_COLS],
                                          start=j == 0, stop=j == TILES - 1)
                mm.then_inc(prob_used, 1)

            def step(k, u):
                if 1 <= k <= BLOCKS and u == 0:
                    b = k - 1
                    pe.wait_ge(top_f32_made, b + 1)
                    pe.wait_ge(s1_row_made, b + 1)
                    for c in range(WIDTH[b] // P):
                        mm = nc.tensor.transpose(aux[:, c * P:(c + 1) * P], top_f32[:, c * P:(c + 1) * P], ident[:, :])
                    mm.then_inc(top_turned, 1)
                if k < BLOCKS and u == PEEL - 1:
                    if k == 0:
                        pe.wait_ge(s1_made, 2)
                    if k >= 1:
                        pe.wait_ge(rows_made, k)
                    if k >= 2:
                        pe.wait_ge(fin_made, FINS * (k - 2) + 1)
                    for i in range(WIDTH[k] // P):
                        c = START[k] // P + i
                        mm = nc.tensor.matmul(aux[:, i * P:(i + 1) * P], s1_scaled[:, c:c + 1].to_broadcast([P, P]),
                                              ident[:, :], start=True, stop=True)
                    mm.then_inc(s1_mm, 1)
                if k >= 2 and u == LAG + 3:
                    b = k - 2
                    pe.wait_ge(numer_copied, b + 1)
                    if k <= BLOCKS:
                        pe.wait_ge(spread_made, k - 1)
                    if b >= 1:
                        pe.wait_ge(fin_made, FINS * (b - 1) + 1)
                    for c in range(WIDTH[b] // P):
                        at = c // CHUNKS_PER_BANK * BANK_COLS + c % CHUNKS_PER_BANK * F_ONES
                        mm = nc.tensor.transpose(aux[:, at:at + F_ONES], numer_out[0:F_ONES, c * P:(c + 1) * P],
                                                 ident[0:F_ONES, 0:F_ONES])
                    mm.then_inc(numer_turned, 1)
                for t in range(2):
                    n = TILES * (k - 1) + 2 * (u - LAG) + t
                    if 0 <= n < TOTAL:
                        shift_less_wall(n)
                        if n % TILES == 0 and n >= TILES:
                            b = n // TILES
                            for i in range(0, WIDTH[b], BANK_COLS):
                                mm = nc.tensor.matmul(aux[:, i:i + BANK_COLS], ones_bf[:, :],
                                                      shift_rows[:, b % 2, i:i + BANK_COLS], start=True, stop=True)
                            mm.then_inc(spread_mm, 1)
                    if 0 <= n - NUMER_LAG < TOTAL:
                        sums(n - NUMER_LAG)
                    if 1 <= k <= BLOCKS and u == 1 and t == 0:
                        b = k - 1
                        pe.wait_ge(cols_made, COLS * (b + 1))
                        for i in range(WIDTH[b] // P):
                            mm = nc.tensor.matmul(aux[0:2, i * P:(i + 1) * P], parts[:, i, :], ident_bf[:, :],
                                                  start=True, stop=True)
                        mm.then_inc(rows_mm, 1)

            for k in range(BLOCKS + 2):
                for u in range(PAIRS if k <= BLOCKS else PEEL):
                    step(k, u)


def kernel(x, adj, L0_gnn_entity_embs, L0_gnn_W, L0_gnn_a):
    import numpy as np
    import concourse.bacc as bacc
    from concourse.bass_utils import run_bass_kernel_spmd

    x, adj, ent, w, a = (np.asarray(v) for v in (x, adj, L0_gnn_entity_embs, L0_gnn_W, L0_gnn_a))
    n_i, n_j = adj.shape
    f = w.shape[1]
    cut = [sum(WIDTHS[:b]) for b in range(len(WIDTHS) + 1)]
    assert cut[-1] == n_i
    arrays = {
        "adj_t": np.concatenate([adj[lo:hi].reshape(hi - lo, n_j // 256, 2, 128).transpose(1, 3, 2, 0).reshape(-1)
                                 for lo, hi in zip(cut, cut[1:])]),
        "x_rows": x.reshape(n_i // 128, 128, f).transpose(1, 0, 2),
        "ent_rows": ent.reshape(n_j // 128, 128, f).transpose(1, 0, 2),
        "w_t": w.T,
        "a_cols": a.reshape(2, f).T,
    }
    arrays = {k: np.ascontiguousarray(v) for k, v in arrays.items()}
    nc = bacc.Bacc("TRN2", target_bir_lowering=False, num_devices=1)
    args = {k: nc.dram_tensor(k, v.shape, mybir.dt.from_np(v.dtype), kind="ExternalInput").ap()
            for k, v in arrays.items()}
    out = nc.dram_tensor("out", (128, n_i // 128, f), F32, kind="ExternalOutput").ap()
    gat_layernorm(nc, out=out, **args)
    r = run_bass_kernel_spmd(nc, [arrays], core_ids=[0])
    return r.results[0]["out"].transpose(1, 0, 2).reshape(n_i, f)
```
